# Optimizing a Trainium2 kernel written in Bass

```python
import numpy as np
import jax
import jax.numpy as jnp

def _softmax(x, axis=-1):
    return jax.nn.softmax(x, axis=axis)

def _gelu(x):
    return jax.nn.gelu(x, approximate=True)

def _silu(x):
    return jax.nn.silu(x)

def _sigmoid(x):
    return jax.nn.sigmoid(x)

def _layernorm(x, axis=-1, eps=1e-05):
    m = jnp.mean(x, axis=axis, keepdims=True)
    v = jnp.var(x, axis=axis, keepdims=True)
    return (x - m) / jnp.sqrt(v + eps)

def _scatter_add(tgt, idx, src, axis=0):
    return tgt.at[idx].add(src)

def _segment_sum(src, seg, n):
    return jax.ops.segment_sum(src, seg, n)
kernel_name = 'mk_gnn_preln_d2_gnn_r8_bb2b6b'

def setup_inputs(seed: int=0):
    np.random.seed(seed)
    _w = jnp.asarray

    def _rec_inputs():
        import jax
        import jax.numpy as jnp
        _gk = jax.random.key(seed)
        x = -0.0003713 + 1 * jax.random.normal(jax.random.fold_in(_gk, 1), (6250, 128), jnp.float32)
        src = jax.random.randint(jax.random.fold_in(_gk, 2), (200000,), 0, 6250, jnp.int32)
        dst = jnp.minimum((6250 * jax.random.uniform(jax.random.fold_in(_gk, 3), (200000,)) ** 2.0).astype(jnp.int32), 49999)
        _o = jnp.argsort(dst, stable=True)
        src = src[_o]
        dst = dst[_o]
        edge_attr_64 = -7.08334e-05 + 0.999895 * jax.random.normal(jax.random.fold_in(_gk, 11), (200000, 64), jnp.float32)
        return (x, src, dst, edge_attr_64)
    x, src, dst, edge_attr_64 = _rec_inputs()

    def _L0_gnn_setup():
        import jax, jax.numpy as jnp
        import numpy as np
        N_NODES = 12500

        def gcn_conv(x, edge_index, W, b):
            n = x.shape[0]
            h = x @ W
            loops = jnp.arange(n, dtype=edge_index.dtype)
            src = jnp.concatenate([edge_index[0], loops])
            dst = jnp.concatenate([edge_index[1], loops])
            ones = jnp.ones(src.shape[0], dtype=h.dtype)
            deg = jax.ops.segment_sum(ones, dst, num_segments=n)
            dinv = jnp.where(deg > 0, jax.lax.rsqrt(deg), 0.0)
            norm = dinv[src] * dinv[dst]
            msg = h[src] * norm[:, None]
            out = jax.ops.segment_sum(msg, dst, num_segments=n)
            return out + b
        key = jax.random.key(seed)
        k1, k2, k3, k4, k5, k6 = jax.random.split(key, 6)
        num_feat, hidden, out_dim = (128, 64, 128)
        x = jax.random.normal(k1, (N_NODES, num_feat), dtype=jnp.float32)
        edge_index = jax.random.randint(k2, (2, 400000), 0, N_NODES, dtype=jnp.int32)
        s1 = 1.0 / np.sqrt(num_feat)
        s2 = 1.0 / np.sqrt(hidden)
        W1 = jax.random.uniform(k3, (num_feat, hidden), jnp.float32, -s1, s1)
        b1 = jnp.zeros((hidden,), jnp.float32)
        W2 = jax.random.uniform(k4, (hidden, out_dim), jnp.float32, -s2, s2)
        b2 = jnp.zeros((out_dim,), jnp.float32)
        return {'x': x, 'edge_index': edge_index, 'W1': W1, 'b1': b1, 'W2': W2, 'b2': b2}
    _L0_gnn_all = _L0_gnn_setup()
    _L0_gnn_in = {k: v for k, v in _L0_gnn_all.items() if k in ('W1', 'b1', 'W2', 'b2')}
    del _L0_gnn_all

    def _L1_gnn_setup():
        import jax, jax.numpy as jnp
        import numpy as np
        N_NODES = 6250
        N_EDGES = 75000
        HIDDEN = 128
        N_RBF = 64
        key = jax.random.key(seed)
        ks = jax.random.split(key, 12)
        s = 1.0 / np.sqrt(HIDDEN)
        sr = 1.0 / np.sqrt(N_RBF)
        return {'h': jax.random.normal(ks[0], (N_NODES, HIDDEN), dtype=jnp.float32), 'rbf': jax.random.normal(ks[1], (N_EDGES, N_RBF), dtype=jnp.float32), 'edge_index': jax.random.randint(ks[2], (2, N_EDGES), 0, N_NODES, dtype=jnp.int64), 'We1': jax.random.uniform(ks[3], (N_RBF, HIDDEN), jnp.float32, -sr, sr), 'be1': jax.random.uniform(ks[4], (HIDDEN,), jnp.float32, -sr, sr), 'We2': jax.random.uniform(ks[5], (HIDDEN, HIDDEN), jnp.float32, -s, s), 'be2': jax.random.uniform(ks[6], (HIDDEN,), jnp.float32, -s, s), 'Wlin': jax.random.uniform(ks[7], (HIDDEN, HIDDEN), jnp.float32, -s, s), 'Wn1': jax.random.uniform(ks[8], (HIDDEN, HIDDEN), jnp.float32, -s, s), 'bn1': jax.random.uniform(ks[9], (HIDDEN,), jnp.float32, -s, s), 'Wn2': jax.random.uniform(ks[10], (HIDDEN, HIDDEN), jnp.float32, -s, s), 'bn2': jax.random.uniform(ks[11], (HIDDEN,), jnp.float32, -s, s)}
    _L1_gnn_all = _L1_gnn_setup()
    _L1_gnn_in = {k: v for k, v in _L1_gnn_all.items() if k in ('We1', 'be1', 'We2', 'be2', 'Wlin', 'Wn1', 'bn1', 'Wn2', 'bn2')}
    del _L1_gnn_all
    return {'x': x, 'src': src, 'dst': dst, 'edge_attr_64': edge_attr_64, 'L0_gnn_W1': _L0_gnn_in['W1'], 'L0_gnn_b1': _L0_gnn_in['b1'], 'L0_gnn_W2': _L0_gnn_in['W2'], 'L0_gnn_b2': _L0_gnn_in['b2'], 'L1_gnn_We1': _L1_gnn_in['We1'], 'L1_gnn_be1': _L1_gnn_in['be1'], 'L1_gnn_We2': _L1_gnn_in['We2'], 'L1_gnn_be2': _L1_gnn_in['be2'], 'L1_gnn_Wlin': _L1_gnn_in['Wlin'], 'L1_gnn_Wn1': _L1_gnn_in['Wn1'], 'L1_gnn_bn1': _L1_gnn_in['bn1'], 'L1_gnn_Wn2': _L1_gnn_in['Wn2'], 'L1_gnn_bn2': _L1_gnn_in['bn2']}

def reference(x, src, dst, edge_attr_64, L0_gnn_W1, L0_gnn_b1, L0_gnn_W2, L0_gnn_b2, L1_gnn_We1, L1_gnn_be1, L1_gnn_We2, L1_gnn_be2, L1_gnn_Wlin, L1_gnn_Wn1, L1_gnn_bn1, L1_gnn_Wn2, L1_gnn_bn2):
    import jax
    import jax.numpy as jnp

    def _L0_gnn_ref(x, edge_index, W1, b1, W2, b2):
        import jax, jax.numpy as jnp
        import numpy as np
        N_NODES = 12500

        def gcn_conv(x, edge_index, W, b):
            n = x.shape[0]
            h = x @ W
            loops = jnp.arange(n, dtype=edge_index.dtype)
            src = jnp.concatenate([edge_index[0], loops])
            dst = jnp.concatenate([edge_index[1], loops])
            ones = jnp.ones(src.shape[0], dtype=h.dtype)
            deg = jax.ops.segment_sum(ones, dst, num_segments=n)
            dinv = jnp.where(deg > 0, jax.lax.rsqrt(deg), 0.0)
            norm = dinv[src] * dinv[dst]
            msg = h[src] * norm[:, None]
            out = jax.ops.segment_sum(msg, dst, num_segments=n)
            return out + b
        h = gcn_conv(x, edge_index, W1, b1)
        h = jax.nn.relu(h)
        out = gcn_conv(h, edge_index, W2, b2)
        return out

    def _L1_gnn_ref(h, rbf, edge_index, We1, be1, We2, be2, Wlin, Wn1, bn1, Wn2, bn2):
        import jax, jax.numpy as jnp
        import numpy as np
        N_NODES = 6250
        N_EDGES = 75000
        HIDDEN = 128
        N_RBF = 64
        src, dst = (edge_index[0], edge_index[1])
        w = jax.nn.silu(rbf @ We1 + be1) @ We2 + be2
        m = w * (h[src] @ Wlin)
        agg = jax.ops.segment_sum(m, dst, num_segments=h.shape[0])
        out = jax.nn.silu(agg @ Wn1 + bn1) @ Wn2 + bn2
        return h + out
    edge_index = jnp.stack([src, dst])
    h = jnp.maximum(_layernorm(x, axis=-1), 0.0)
    x = x + _L0_gnn_ref(h, edge_index, L0_gnn_W1, L0_gnn_b1, L0_gnn_W2, L0_gnn_b2)
    h = jnp.maximum(_layernorm(x, axis=-1), 0.0)
    x = x + _L1_gnn_ref(h, edge_attr_64, edge_index, L1_gnn_We1, L1_gnn_be1, L1_gnn_We2, L1_gnn_be2, L1_gnn_Wlin, L1_gnn_Wn1, L1_gnn_bn1, L1_gnn_Wn2, L1_gnn_bn2)
    return x

_drawn_inputs = setup_inputs


def setup_inputs(seed=0):
    import zlib

    import numpy as np

    out = dict(_drawn_inputs(seed))
    spreads = {'L0_gnn_b1': (0.0, 0.1), 'L0_gnn_b2': (0.0, 0.1)}
    factors = {'L1_gnn_bn1': 5.571}
    for name, (base, spread) in spreads.items():
        noise = np.random.default_rng([zlib.crc32(name.encode()), seed]).standard_normal(out[name].shape)
        drawn = base * np.exp(spread * noise) if base else spread * noise
        out[name] = jnp.asarray(drawn.astype(out[name].dtype))
    for name, factor in factors.items():
        out[name] = (out[name] * factor).astype(out[name].dtype)
    return out
```

```python
import concourse.bass as bass
from concourse import mybir
from contextlib import ExitStack

fp32 = mybir.dt.float32
bf16 = mybir.dt.bfloat16
int32 = mybir.dt.int32
ALU = mybir.AluOpType
ACT = mybir.ActivationFunctionType
AX = mybir.AxisListType

P = 128
N_NODES, N_EDGES = 6250, 200000
F, HID, RBF = 128, 64, 64
NB = -(-N_NODES // P)
LAST_ROWS = N_NODES - (NB - 1) * P
CB = 7
CHUNKS = NB // CB
U = 8
GE = P * U
G = -(-N_EDGES // GE)
RING = 4
ITERS = G // RING
HALVES = -(-G // P)
FULL1 = N_EDGES // GE - P
TAIL = N_EDGES - (P + FULL1) * GE
PAD_DST = NB * P - 1
PARTS = 3
TW = PARTS * HID
EPS = 1e-5
assert NB == CHUNKS * CB and G == ITERS * RING and TAIL % U == 0 and TAIL > 0
assert N_NODES <= PAD_DST


def gnn_kernel(nc, x, src, dst, edge_attr, W1, b1, W2, b2, We1, be1, We2, be2, Wlin, Wn1, bn1, Wn2, bn2, out):
    ctx = ExitStack()
    with ctx:
        def sb(name, shape, dt):
            return ctx.enter_context(nc.sbuf_tensor(name, shape, dt))

        def sem(name):
            return ctx.enter_context(nc.semaphore(name))

        gcn_table = [nc.dram_tensor(f"gcn_table{i}", (NB * P, TW), bf16, kind="Internal").ap() for i in range(2)]
        lin_table = nc.dram_tensor("lin_table", (NB * P, F), fp32, kind="Internal").ap()

        ident = sb("ident", [P, P], fp32)
        iota_i = sb("iota_i", [P, P], int32)
        iota_f = sb("iota_f", [P, P], fp32)
        iota_u = sb("iota_u", [P, P, U], bf16)
        base_i = sb("base_i", [P, NB], int32)
        neg_base = sb("neg_base", [P, NB], fp32)
        eps_col = sb("eps_col", [P, 1], fp32)
        ones3 = sb("ones3", [PARTS, P], bf16)
        zeros_b = sb("zeros_b", [P, P], bf16)
        w1_sb = sb("w1_sb", [P, HID], fp32)
        w2_sb = sb("w2_sb", [HID, F], fp32)
        we1_sb = sb("we1_sb", [P, F], fp32)
        we2_sb = sb("we2_sb", [P, F], fp32)
        wlin_sb = sb("wlin_sb", [P, F], fp32)
        wn1_sb = sb("wn1_sb", [P, F], fp32)
        wn2_sb = sb("wn2_sb", [P, F], fp32)
        be1_col = sb("be1_col", [P, 1], fp32)
        bn1_col = sb("bn1_col", [P, 1], fp32)
        b1_all = sb("b1_all", [P, HID], fp32)
        b2_all = sb("b2_all", [P, F], fp32)
        bn2_all = sb("bn2_all", [P, F], fp32)
        be2_rows = sb("be2_rows", [PARTS, F], fp32)
        be2_hi = sb("be2_hi", [PARTS, F], bf16)
        be2_mid = sb("be2_mid", [PARTS, F], bf16)
        be2_lo = sb("be2_lo", [PARTS, F], bf16)
        be2_res = sb("be2_res", [PARTS, F], fp32)
        be2_parts = sb("be2_parts", [PARTS, 4, F], bf16)

        xr = sb("xr", [P, NB, F], fp32)
        agg = sb("agg", [P, NB * TW], fp32)
        agg_gcn = agg[:, :].rearrange("p (b c) -> p b c", b=NB)
        agg_lin = agg[:, 0:NB * F].rearrange("p (b c) -> p b c", b=NB)
        tmsg = sb("tmsg", [P, NB, HID], fp32)
        table_sb = sb("table_sb", [P, CB, TW], bf16)
        dinv = sb("dinv", [P, NB], fp32)
        deg_sb = sb("deg_sb", [P, NB], fp32)

        raw_d = sb("raw_d", [P, HALVES, GE], int32)
        raw_s = sb("raw_s", [P, HALVES, GE], int32)
        raw_f = sb("raw_f", [P, HALVES, GE], fp32)
        NC = HALVES * P * U
        idx_all = sb("idx_all", [P, NC], int32)
        dst_f = sb("dst_f", [P, NC], fp32)
        dst_i = raw_s[:, :, :].rearrange("p k e -> p (k e)")
        tmp_i = raw_d[:, :, :].rearrange("p k e -> p (k e)")
        dlo = sb("dlo", [P, NC], bf16)
        dhi = sb("dhi", [P, NC], bf16)
        mm_i = sb("mm_i", [P, 2 * HALVES], int32)
        mm_f = sb("mm_f", [P, 2 * HALVES], fp32)
        bounds = sb("bounds", [1, 2 * HALVES * P], int32)

        idx = sb("idx", [P, RING, U], int32)
        gat = sb("gat", [P, RING, U, F], fp32)
        gat_b = gat[:, :, :, :].rearrange("p s u f -> p s (u f)").bitcast(bf16)
        ea = sb("ea", [P, RING, U * RBF], fp32)
        hch_in = sb("hch_in", [P, CB, HID], fp32)
        hot_lo = sb("hot_lo", [P, 2, P, U], bf16)
        hot_hi = sb("hot_hi", [P, 2, NB, U], bf16)
        dl_b = sb("dl_b", [P, U], bf16)
        dl_f = sb("dl_f", [P, U], fp32)
        hot_f = sb("hot_f", [P, U, P], fp32)
        ea_t = sb("ea_t", [P, 4 * P], fp32)
        act_t = sb("act_t", [P, 2, 4 * P], fp32)
        msg = sb("msg", [P, 2, 4, F], fp32)

        c0 = sb("c0", [P, CB, F], fp32)
        c1 = sb("c1", [P, CB, F], fp32)
        hch = sb("hch", [P, CB, F], fp32)
        cht = sb("cht", [P, CB, P], fp32)
        st = sb("st", [P, 4, CB], fp32)

        pa = ctx.enter_context(nc.psum_tensor("pa", [P, 2, 512], fp32))
        pb = ctx.enter_context(nc.psum_tensor("pb", [P, 2, 512], fp32))
        pc = ctx.enter_context(nc.psum_tensor("pc", [P, 512], fp32))
        pd = ctx.enter_context(nc.psum_tensor("pd", [P, 512], fp32))
        pa_f = pa[:, :, :].rearrange("p a b -> p (a b)")
        pb_f = pb[:, :, :].rearrange("p a b -> p (a b)")
        banks = [pa[:, 0, :], pa[:, 1, :], pb[:, 0, :], pb[:, 1, :]]
        deg_ps = pd[:, 0:NB]
        row_ps = pc[0:1, :]

        raw_set = sem("raw_set")
        raw_loaded = sem("raw_loaded")
        x_loaded = sem("x_loaded")
        w_loaded = sem("w_loaded")
        pool_consts = sem("pool_consts")
        consts = sem("consts")
        dve_done = sem("dve_done")
        act_done = sem("act_done")
        raw_fp = sem("raw_fp")
        turned = sem("turned")
        turned_out = sem("turned_out")
        mm_ready = sem("mm_ready")
        row_ready = sem("row_ready")
        bounds_ready = sem("bounds_ready")
        hist_hot = sem("hist_hot")
        hist_used = sem("hist_used")
        deg_ready = sem("deg_ready")

        class Node:
            def __init__(self, n):
                self.var = sem(f"{n}_var")
                self.std = sem(f"{n}_std")
                self.h = sem(f"{n}_h")
                self.turned = sem(f"{n}_turned")
                self.ht = sem(f"{n}_ht")
                self.mm = sem(f"{n}_mm")
                self.out = sem(f"{n}_out")
                self.stored = sem(f"{n}_stored")
        ln1, lin2, ln2 = Node("ln1"), Node("lin2"), Node("ln2")
        up, down = Node("up"), Node("down")
        split_ready = [sem(f"split_ready{i}") for i in range(2)]
        table_stored = [sem(f"table_stored{i}") for i in range(2)]
        out_stored = sem("out_stored")

        class Pass:
            def __init__(self, n):
                self.idx_ready = sem(f"{n}_idx_ready")
                self.gathered = [sem(f"{n}_gathered{s}") for s in range(RING)]
                self.rows_used = sem(f"{n}_rows_used")
                self.hot = sem(f"{n}_hot")
                self.summed = sem(f"{n}_summed")
                self.added = sem(f"{n}_added")
        gcn = [Pass("gcn0"), Pass("gcn1")]
        lin = Pass("lin")
        ea_loaded = [sem(f"ea_loaded{s}") for s in range(RING)]
        ea_turned = sem("ea_turned")
        ea_out = sem("ea_out")
        hid_mm = sem("hid_mm")
        hid_act = sem("hid_act")
        w_mm = sem("w_mm")
        msg_ready = sem("msg_ready")

        passed = sem("passed")

        N_W = 17
        block = ctx.enter_context(nc.Block())

        def first_block(eng, g):
            return eng.value_load(bounds[0:1, bass.ds(g, 1)], min_val=0, max_val=NB - 1)

        def end_block(eng, g):
            return eng.value_load(bounds[0:1, bass.ds(g + HALVES * P, 1)], min_val=1, max_val=NB)

        @block.sync
        def _(sp):
            sp.wait_ge(raw_set, 2)
            for raw, arr in ((raw_d, dst), (raw_s, src)):
                sp.dma_start(raw[:, 0, :], arr[0:P * GE].rearrange("(p e) -> p e", e=GE)).then_inc(raw_loaded, 16)
                sp.dma_start(raw[0:FULL1, 1, :],
                             arr[P * GE:(P + FULL1) * GE].rearrange("(p e) -> p e", e=GE)).then_inc(raw_loaded, 16)
                sp.dma_start(raw[FULL1:FULL1 + 1, 1, 0:TAIL],
                             arr[(P + FULL1) * GE:N_EDGES].rearrange("(p e) -> p e", p=1)).then_inc(raw_loaded, 16)
            sp.wait_ge(raw_set, 3)
            sp.dma_start(xr[:, 0:NB - 1, :], x[0:(NB - 1) * P, :].rearrange("(b p) f -> p b f", p=P)).then_inc(x_loaded, 16)
            sp.dma_start(xr[0:LAST_ROWS, NB - 1, :], x[(NB - 1) * P:N_NODES, :]).then_inc(x_loaded, 16)

            def row(v, n):
                return v.rearrange("(a n) -> a n", a=1).to_broadcast([n, v.shape[0]])
            loads = [(w1_sb[:, :], W1), (w2_sb[:, :], W2), (we1_sb[0:RBF, :], We1), (we1_sb[RBF:2 * RBF, :], We1),
                     (we2_sb[:, :], We2), (wlin_sb[:, :], Wlin), (wn1_sb[:, :], Wn1), (wn2_sb[:, :], Wn2),
                     (be1_col[:, :], be1.rearrange("(p a) -> p a", a=1)),
                     (bn1_col[:, :], bn1.rearrange("(p a) -> p a", a=1)),
                     (b1_all[:, :], row(b1, P)), (b2_all[:, :], row(b2, P)), (bn2_all[:, :], row(bn2, P)),
                     (be2_rows[:, :], row(be2, PARTS))]
            assert len(loads) == N_W - 3
            for to, of in loads:
                sp.dma_start(to, of).then_inc(w_loaded, 16)

            for i in range(2):
                rows = gcn_table[i].rearrange("(b p) c -> p b c", p=P)
                with sp.Fori(0, CHUNKS) as c:
                    sp.wait_ge(split_ready[i], c + 1)
                    sp.dma_start(rows[:, bass.ds(c * CB, CB), :], table_sb[:, :, :]).then_inc(table_stored[i], 16)
            rows = lin_table.rearrange("(b p) c -> p b c", p=P)
            with sp.Fori(0, CHUNKS) as c:
                sp.wait_ge(ln2.out, c + 1)
                sp.dma_start(rows[:, bass.ds(c * CB, CB), :], c1[:, :, :]).then_inc(ln2.stored, 16)

            def load_ea(g, s):
                rows = edge_attr[bass.ds(g * GE, GE), :].rearrange("(p u) f -> p (u f)", u=U)
                sp.dma_start(ea[:, s, :], rows).then_inc(ea_loaded[s], 16)
            for s in range(RING):
                load_ea(s, s)
            with sp.Fori(1, ITERS - 1) as it:
                for s in range(RING):
                    sp.wait_ge(ea_turned, it * RING + (s - RING + 1))
                    load_ea(it * RING + s, s)
            for s in range(RING):
                g = (ITERS - 1) * RING + s
                sp.wait_ge(ea_turned, g - RING + 1)
                if g < G - 1:
                    load_ea(g, s)
                else:
                    sp.dma_start(ea[0:TAIL // U, s, :],
                                 edge_attr[g * GE:N_EDGES, :].rearrange("(p u) f -> p (u f)", u=U)).then_inc(ea_loaded[s], 16)

            with sp.Fori(0, CHUNKS - 1) as c:
                sp.wait_ge(down.out, c + 1)
                sp.dma_start(out[bass.ds(c * (CB * P), CB * P), :].rearrange("(b p) f -> p b f", p=P),
                             c1[:, :, :]).then_inc(out_stored, 16)
            sp.wait_ge(down.out, CHUNKS)
            sp.dma_start(out[(NB - CB) * P:(NB - 1) * P, :].rearrange("(b p) f -> p b f", p=P),
                         c1[:, 0:CB - 1, :]).then_inc(out_stored, 16)
            sp.dma_start(out[(NB - 1) * P:N_NODES, :], c1[0:LAST_ROWS, CB - 1, :]).then_inc(out_stored, 16)
            sp.wait_ge(out_stored, 16 * (CHUNKS + 1))

        @block.gpsimd
        def _(pool):
            pool.memset(raw_d[:, 1, :], PAD_DST).then_inc(raw_set, 1)
            pool.memset(raw_s[:, 1, :], 0).then_inc(raw_set, 1)
            pool.memset(xr[:, NB - 1, :], 0.0).then_inc(raw_set, 1)
            pool.iota(iota_i[:, :], pattern=[[1, P]], base=0, channel_multiplier=0).then_inc(pool_consts, 1)
            pool.iota(base_i[:, :], pattern=[[-P, NB]], base=0, channel_multiplier=0).then_inc(pool_consts, 1)
            pool.memset(ident[:, :], 0.0).then_inc(pool_consts, 1)
            pool.memset(ones3[:, :], 1.0).then_inc(pool_consts, 1)
            pool.memset(zeros_b[:, :], 0.0).then_inc(pool_consts, 1)
            pool.memset(eps_col[:, :], EPS).then_inc(pool_consts, 1)
            pool.memset(ea[:, :, :], 0.0).then_inc(pool_consts, 1)
            pool.wait_ge(pool_consts, 7)
            pool.affine_select(out=ident[:, :], in_=ident[:, :], compare_op=ALU.not_equal, fill=1.0, base=0,
                               pattern=[[-1, P]], channel_multiplier=1).then_inc(pool_consts, 1)

            def gather(ps, table, dest, s):
                for j in range(U):
                    pool.indirect_dma_start(
                        out=dest(s, j), out_offset=None, in_=table,
                        in_offset=bass.IndirectOffsetOnAxis(ap=idx[:, s, j:j + 1], axis=0)).then_inc(ps.gathered[s], 16)

            def edge_pass(ps, table, dest):
                for s in range(RING):
                    pool.wait_ge(ps.idx_ready, s + 1)
                    gather(ps, table, dest, s)
                with pool.Fori(1, ITERS) as it:
                    for s in range(RING):
                        pool.wait_ge(ps.idx_ready, it * RING + (s + 1))
                        pool.wait_ge(ps.rows_used, it * RING + (s - RING + 1))
                        pool.sem_inc(passed, 1)
                        gather(ps, table, dest, s)

            for i in range(2):
                pool.wait_ge(table_stored[i], 16 * CHUNKS)
                edge_pass(gcn[i], gcn_table[i], lambda s, j: gat_b[:, s, j * TW:(j + 1) * TW])
            pool.wait_ge(ln2.stored, 16 * CHUNKS)
            edge_pass(lin, lin_table, lambda s, j: gat[:, s, j, :])

        @block.scalar
        def _(act):
            mine = act.alloc_register("act_steps")
            act.reg_mov(mine, 0)

            def step(ins):
                ins.then_inc(act_done, 1)
                act.reg_add(mine, mine, 1)
                act.wait_ge(act_done, mine)

            act.wait_ge(raw_loaded, 16 * 6)
            act.wait_ge(turned, 4)
            act.activation(raw_f[:, :, :], raw_s[:, :, :], ACT.Copy).then_inc(raw_fp, 1)

            def transposes_out(nd, c, n):
                act.wait_ge(nd.turned, c + 1)
                act.wait_ge(nd.mm, c)
                act.activation(cht[0:n, :, :], pa_f[0:n, 0:CB * P].rearrange("p (b q) -> p b q", q=P),
                               ACT.Copy).then_inc(nd.ht, 1)

            def std(nd, c):
                act.wait_ge(nd.var, c + 1)
                act.activation(st[:, 2, :], st[:, 1, :], ACT.Sqrt, bias=eps_col[:, :], scale=1.0 / F).then_inc(nd.std, 1)

            act.wait_ge(pool_consts, 8)
            with act.Fori(0, CHUNKS) as c:
                std(ln1, c)
                transposes_out(ln1, c, P)
                act.wait_ge(ln1.mm, c + 1)
                act.activation(tmsg[:, bass.ds(c * CB, CB), :],
                               pb[:, 0, 0:CB * HID].rearrange("p (b q) -> p b q", q=HID), ACT.Copy).then_inc(ln1.out, 1)
            act.wait_ge(deg_ready, 1)
            act.activation(deg_sb[:, :], deg_ps, ACT.Sqrt, bias=1.0).then_inc(deg_ready, 1)

            def next_idx(ps, g, s):
                act.activation(idx[:, s, :], idx_all[:, bass.ds(g * U, U)], ACT.Copy).then_inc(ps.idx_ready, 1)

            def first_idx(ps):
                for s in range(RING):
                    next_idx(ps, s, s)

            def after_gather(ps, it, s):
                act.wait_ge(ps.gathered[s], (it + 1) * (16 * U))
                next_idx(ps, (it + 1) * RING + s, s)

            for i in range(2):
                first_idx(gcn[i])
                with act.Fori(0, ITERS - 1) as it:
                    for s in range(RING):
                        after_gather(gcn[i], it, s)
                if i == 1:
                    break
                for s in range(RING):
                    act.wait_ge(gcn[i].gathered[s], ITERS * 16 * U)
            for s in range(RING):
                act.wait_ge(gcn[1].gathered[s], ITERS * 16 * U)

            with act.Fori(0, CHUNKS) as c:
                transposes_out(lin2, c, HID)
                std(ln2, c)
                transposes_out(ln2, c, P)
                act.wait_ge(ln2.mm, c + 1)
                act.wait_ge(ln2.stored, c * 16)
                act.activation(c1[:, :, :], pb_f[:, 0:CB * F].rearrange("p (b q) -> p b q", q=F),
                               ACT.Copy).then_inc(ln2.out, 1)

            def edge_act(g):
                act.wait_ge(ea_turned, g + 1)
                act.wait_ge(hid_mm, g)
                act.activation(ea_t[:, :], pd[:, :], ACT.Copy).then_inc(ea_out, 1)
                act.wait_ge(hid_mm, g + 1)
                act.wait_ge(w_mm, g)
                act.activation(act_t[:, :, :], pa[:, :, :], ACT.Silu, bias=be1_col[:, :]).then_inc(hid_act, 1)

            first_idx(lin)
            edge_act(0)
            with act.Fori(0, ITERS - 1) as it:
                for s in range(RING):
                    edge_act(it * RING + (s + 1))
                    after_gather(lin, it, s)
            for s in range(RING - 1):
                edge_act((ITERS - 1) * RING + s + 1)

            with act.Fori(0, CHUNKS) as c:
                transposes_out(up, c, P)
                act.wait_ge(up.mm, c + 1)
                act.wait_ge(down.mm, c)
                act.activation(hch[:, :, :], pb_f[:, 0:CB * P].rearrange("p (b q) -> p b q", q=P), ACT.Silu,
                               bias=bn1_col[:, :]).then_inc(up.out, 1)

        @block.vector
        def _(dve):
            mine = dve.alloc_register("dve_steps")
            dve.reg_mov(mine, 0)

            def step(ins):
                ins.then_inc(dve_done, 1)
                dve.reg_add(mine, mine, 1)
                dve.wait_ge(dve_done, mine)

            def bc(ap, n):
                return ap.rearrange("p (b a) -> p b a", a=1).to_broadcast([P, ap.shape[1], n])

            def lanes(t, g, n):
                return t[:, bass.ds(g * U, U)].rearrange("p (a u) -> p a u", a=1).to_broadcast([P, n, U])

            dve.wait_ge(pool_consts, 7)
            step(dve.tensor_copy(iota_f[:, :], iota_i[:, :]))
            step(dve.tensor_copy(iota_u[:, :, :], bc(iota_i[:, :], U)))
            step(dve.tensor_copy(neg_base[:, :], base_i[:, :]))
            step(dve.memset(agg[:, :], 0.0))

            dve.wait_ge(raw_loaded, 16 * 6)
            dve.tensor_copy(raw_f[:, :, :], raw_d[:, :, :]).then_inc(raw_fp, 1)
            step(dve.tensor_reduce(mm_i[:, 0:HALVES], raw_d[:, :, :], AX.X, ALU.min))
            step(dve.tensor_reduce(mm_i[:, HALVES:2 * HALVES], raw_d[:, :, :], AX.X, ALU.max))
            step(dve.tensor_scalar(mm_i[:, :], mm_i[:, :], 7, None, ALU.arith_shift_right))
            step(dve.tensor_copy(mm_f[:, :], mm_i[:, :]))
            dve.tensor_scalar(mm_f[:, HALVES:2 * HALVES], mm_f[:, HALVES:2 * HALVES], 1.0, None, ALU.add).then_inc(mm_ready, 1)
            dve.wait_ge(row_ready, 1)
            dve.tensor_copy(bounds[:, :], row_ps).then_inc(bounds_ready, 1)

            def turned_copy(n, to):
                k, q = n // 2, n % 2
                view = to[:, k * GE:(k + 1) * GE].rearrange("p (g j) -> p j g", j=U)[:, 4 * q:4 * q + 4, :]
                dve.wait_ge(turned, len(seen) + 1)
                seen.append(n)
                dve.tensor_copy(view, banks[n].rearrange("p (j g) -> p j g", g=P)).then_inc(turned_out, 1)
            seen = []
            for n in range(4):
                turned_copy(n, dst_f[:, :])
            for n in range(4):
                turned_copy(n, idx_all[:, :])
            dve.wait_ge(turned_out, 8)
            step(dve.tensor_copy(dst_i, dst_f[:, :]))
            step(dve.tensor_scalar(tmp_i, dst_i, P - 1, None, ALU.bitwise_and))
            step(dve.tensor_copy(dlo[:, :], tmp_i))
            step(dve.tensor_scalar(tmp_i, dst_i, 7, None, ALU.arith_shift_right))
            step(dve.tensor_copy(dhi[:, :], tmp_i))

            dve.wait_ge(w_loaded, 16 * (N_W - 3))
            dve.wait_ge(pool_consts, 8)
            step(dve.tensor_copy(be2_hi[:, :], be2_rows[:, :]))
            step(dve.tensor_tensor(be2_res[:, :], be2_rows[:, :], be2_hi[:, :], ALU.subtract))
            step(dve.tensor_copy(be2_mid[:, :], be2_res[:, :]))
            step(dve.tensor_tensor(be2_lo[:, :], be2_res[:, :], be2_mid[:, :], ALU.subtract))
            step(dve.tensor_scalar(be2_res[:, :], be2_hi[:, :], ident[0:PARTS, 0:1], None, ALU.mult))
            step(dve.scalar_tensor_tensor(be2_res[:, :], be2_mid[:, :], ident[0:PARTS, 1:2], be2_res[:, :], ALU.mult, ALU.add))
            step(dve.scalar_tensor_tensor(be2_res[:, :], be2_lo[:, :], ident[0:PARTS, 2:3], be2_res[:, :], ALU.mult, ALU.add))
            for i in range(4):
                dve.tensor_copy(be2_parts[:, i, :], be2_res[:, :]).then_inc(consts, 1)

            def layernorm_relu(nd, c, rows):
                step(dve.tensor_reduce(st[:, 0, :], rows, AX.X, ALU.add))
                step(dve.tensor_scalar(st[:, 0, :], st[:, 0, :], -1.0 / F, None, ALU.mult))
                step(dve.tensor_tensor(c0[:, :, :], rows, bc(st[:, 0, :], F), ALU.add))
                step(dve.tensor_tensor(cht_sq[:, :, :], c0[:, :, :], c0[:, :, :], ALU.mult))
                dve.tensor_reduce(st[:, 1, :], cht_sq[:, :, :], AX.X, ALU.add).then_inc(nd.var, 1)
                dve.wait_ge(nd.std, c + 1)
                step(dve.reciprocal(st[:, 3, :], st[:, 2, :]))
                dve.wait_ge(nd.turned, c)
                dve.scalar_tensor_tensor(hch[:, :, :], c0[:, :, :], 0.0, bc(st[:, 3, :], F), ALU.max, ALU.mult).then_inc(nd.h, 1)
                dve.wait_ge(nd.h, c + 1)
            cht_sq = gat[:, :, :, :].rearrange("p s u f -> p (s u) f")[:, 0:CB, :]

            dve.wait_ge(x_loaded, 32)
            with dve.Fori(0, CHUNKS) as c:
                layernorm_relu(ln1, c, xr[:, bass.ds(c * CB, CB), :])

            with dve.Fori(0, ITERS * RING // 2) as it:
                for s in range(2):
                    g = it * 2 + s
                    dve.wait_ge(hist_used, it * 2 + s)
                    dve.tensor_tensor(hot_lo[:, s, :, :], iota_u[:, :, :], lanes(dlo, g, P), ALU.is_equal)\
                       .then_inc(hist_hot, 1)
                    dve.tensor_tensor(hot_hi[:, s, :, :], iota_u[:, 0:NB, :], lanes(dhi, g, NB), ALU.is_equal)\
                       .then_inc(hist_hot, 1)
            dve.wait_ge(deg_ready, 2)
            step(dve.reciprocal(dinv[:, :], deg_sb[:, :]))
            dve.sem_inc(passed, 1)

            def split_out(i, c, tm):
                dve.wait_ge(table_stored[i], c * 16)
                dve.sem_inc(passed, 1)
                step(dve.tensor_copy(table_sb[:, :, 0:HID], tm))
                step(dve.tensor_tensor(c0[:, :, 0:HID], tm, table_sb[:, :, 0:HID], ALU.subtract))
                step(dve.tensor_copy(table_sb[:, :, HID:2 * HID], c0[:, :, 0:HID]))
                dve.tensor_tensor(table_sb[:, :, 2 * HID:3 * HID], c0[:, :, 0:HID], table_sb[:, :, HID:2 * HID],
                                  ALU.subtract).then_inc(split_ready[i], 1)
                dve.wait_ge(split_ready[i], c + 1)

            dve.wait_ge(ln1.out, CHUNKS)
            with dve.Fori(0, CHUNKS) as c:
                tm = tmsg[:, bass.ds(c * CB, CB), :]
                step(dve.tensor_tensor(tm, tm, bc(dinv[:, bass.ds(c * CB, CB)], HID), ALU.mult))
                split_out(0, c, tm)

            pairs = dve.alloc_register("pairs_dve")
            dve.wait_ge(bounds_ready, 1)

            def gcn_pass(ps):
                dve.reg_mov(pairs, 0)
                with dve.Fori(0, G) as g:
                    first, end = first_block(dve, g), end_block(dve, g)
                    with dve.Fori(first, end) as b:
                        step(dve.tensor_scalar(dl_b[:, :], dst_f[:, bass.ds(g * U, U)], neg_base[:, bass.ds(b, 1)], None, ALU.add))
                        dve.tensor_tensor(hot_lo[:, 0, :, :], iota_u[:, :, :],
                                          dl_b[:, :].rearrange("p (a u) -> p a u", a=1).to_broadcast([P, P, U]),
                                          ALU.is_equal).then_inc(ps.hot, 1)
                        dve.reg_add(pairs, pairs, 1)
                        dve.wait_ge(ps.summed, pairs)
                        a = agg_gcn[:, bass.ds(b, 1), :].rearrange("p a c -> p (a c)")
                        dve.tensor_tensor(a, a, pc[:, 0:TW], ALU.add).then_inc(ps.added, 1)
                    dve.sem_inc(ps.rows_used, 1)
                dve.wait_ge(ps.added, pairs)
                dve.sem_inc(passed, 1)

            gcn_pass(gcn[0])

            def gcn_sum(c):
                blocks = bass.ds(c * CB, CB)
                a = agg_gcn[:, blocks, :]
                tm = tmsg[:, blocks, :]
                step(dve.tensor_tensor(c0[:, :, 0:HID], a[:, :, 0:HID], a[:, :, HID:2 * HID], ALU.add))
                step(dve.tensor_tensor(c0[:, :, 0:HID], c0[:, :, 0:HID], a[:, :, 2 * HID:3 * HID], ALU.add))
                step(dve.tensor_tensor(c0[:, :, 0:HID], c0[:, :, 0:HID], tm, ALU.add))
                step(dve.tensor_tensor(c0[:, :, 0:HID], c0[:, :, 0:HID], bc(dinv[:, blocks], HID), ALU.mult))
                return tm, a

            def all_rows(ap):
                return ap.rearrange("p (a n) -> p a n", a=1).to_broadcast([P, CB, ap.shape[1]])

            with dve.Fori(0, CHUNKS) as c:
                tm, a = gcn_sum(c)
                step(dve.tensor_tensor(c0[:, :, 0:HID], c0[:, :, 0:HID], all_rows(b1_all[:, :]), ALU.add))
                step(dve.scalar_tensor_tensor(tm, c0[:, :, 0:HID], 0.0, bc(dinv[:, bass.ds(c * CB, CB)], HID), ALU.max, ALU.mult))
                split_out(1, c, tm)
            step(dve.memset(agg[:, :], 0.0))
            dve.sem_inc(passed, 1)

            gcn_pass(gcn[1])

            with dve.Fori(0, CHUNKS) as c:
                rows = xr[:, bass.ds(c * CB, CB), :]
                tm, a = gcn_sum(c)
                dve.wait_ge(lin2.turned, c)
                dve.tensor_copy(hch_in[:, :, :], c0[:, :, 0:HID]).then_inc(lin2.h, 1)
                step(dve.tensor_tensor(rows, rows, all_rows(b2_all[:, :]), ALU.add))
                dve.wait_ge(lin2.mm, c + 1)
                step(dve.tensor_tensor(rows, rows, pb_f[:, 0:CB * F].rearrange("p (b q) -> p b q", q=F), ALU.add))
                dve.sem_inc(lin2.out, 1)
                layernorm_relu(ln2, c, rows)
                step(dve.tensor_tensor(rows, rows, hch[:, :, :], ALU.add))
                step(dve.tensor_tensor(rows, rows, all_rows(bn2_all[:, :]), ALU.add))
            step(dve.memset(agg[:, 0:NB * F], 0.0))
            dve.sem_inc(passed, 1)

            dve.reg_mov(pairs, 0)

            def lin_group(g, it, s):
                first, end = first_block(dve, g), end_block(dve, g)
                dve.wait_ge(w_mm, g + 1)
                dve.wait_ge(lin.gathered[s], (it + 1) * (16 * U))
                rows = gat[:, s, :, :].rearrange("p (i h) f -> p h i f", h=2)
                for h in range(2):
                    dve.tensor_tensor(msg[:, h, :, :], pb[:, h, :].rearrange("p (i f) -> p i f", f=F),
                                      rows[:, h, :, :], ALU.mult).then_inc(msg_ready, 1)
                dve.wait_ge(msg_ready, g * 2 + 2)
                dve.sem_inc(lin.rows_used, 1)
                with dve.Fori(first, end) as b:
                    step(dve.tensor_scalar(dl_f[:, :], dst_f[:, bass.ds(g * U, U)], neg_base[:, bass.ds(b, 1)], None, ALU.add))
                    dve.tensor_tensor(hot_f[:, :, :], iota_f[:, :].rearrange("p (a d) -> p a d", a=1).to_broadcast([P, U, P]),
                                      bc(dl_f[:, :], P), ALU.is_equal).then_inc(lin.hot, 1)
                    dve.reg_add(pairs, pairs, 1)
                    dve.wait_ge(lin.summed, pairs)
                    a = agg_lin[:, bass.ds(b, 1), :].rearrange("p a c -> p (a c)")
                    dve.tensor_tensor(a, a, pc[:, 0:F], ALU.add).then_inc(lin.added, 1)

            with dve.Fori(0, ITERS) as it:
                for s in range(RING):
                    lin_group(it * RING + s, it, s)
            dve.wait_ge(lin.added, pairs)
            dve.sem_inc(passed, 1)

            with dve.Fori(0, CHUNKS) as c:
                blocks = bass.ds(c * CB, CB)
                dve.wait_ge(up.turned, c)
                dve.sem_inc(passed, 1)
                dve.tensor_copy(c0[:, :, :], agg_lin[:, blocks, :]).then_inc(up.h, 1)
                dve.wait_ge(down.mm, c + 1)
                dve.wait_ge(out_stored, c * 16)
                dve.tensor_tensor(c1[:, :, :], xr[:, blocks, :], pa_f[:, 0:CB * F].rearrange("p (b q) -> p b q", q=F),
                                  ALU.add).then_inc(down.out, 1)

        @block.tensor
        def _(pe):
            pe.wait_ge(pool_consts, 8)
            for a in range(2):
                pe.wait_ge(raw_fp, a + 1)
                for k in range(HALVES):
                    for q in range(2):
                        n = 2 * k + q
                        if a == 1:
                            pe.wait_ge(turned_out, n + 1)
                        cols = raw_f[:, k, :].rearrange("p (g j) -> p j g", j=U)
                        for j in range(4):
                            last = pe.transpose(banks[n][:, j * P:(j + 1) * P], cols[:, 4 * q + j, :], ident[:, :])
                        last.then_inc(turned, 1)
                if a == 0:
                    pe.wait_ge(mm_ready, 1)
                    for i in range(2 * HALVES):
                        last = pe.matmul(pc[0:1, i * P:(i + 1) * P], mm_f[:, i:i + 1], ident[:, :], start=True, stop=True)
                    last.then_inc(row_ready, 1)

            def turn(nd, c, rows, n):
                pe.wait_ge(nd.h, c + 1)
                pe.wait_ge(nd.ht, c)
                pe.sem_inc(passed, 1)
                for j in range(CB):
                    last = pe.transpose(pa_f[0:n, j * P:(j + 1) * P], rows(j), ident[:, :])
                last.then_inc(nd.turned, 1)

            pe.wait_ge(w_loaded, 16 * (N_W - 3))
            pe.wait_ge(turned_out, 8)
            with pe.Fori(0, CHUNKS) as c:
                turn(ln1, c, lambda j: hch[:, j, :], P)
                pe.wait_ge(ln1.ht, c + 1)
                pe.wait_ge(ln1.out, c)
                for j in range(CB):
                    last = pe.matmul(pb[:, 0, j * HID:(j + 1) * HID], cht[:, j, :], w1_sb[:, :], start=True, stop=True)
                last.then_inc(ln1.mm, 1)

            pe.matmul(deg_ps, zeros_b[:, :], zeros_b[:, 0:NB], start=True, stop=False).then_inc(hist_used, 1)
            with pe.Fori(0, ITERS * RING // 2) as it:
                for s in range(2):
                    pe.wait_ge(hist_hot, (it * 2 + s) * 2 + 2)
                    for u in range(U):
                        last = pe.matmul(deg_ps, hot_lo[:, s, :, u], hot_hi[:, s, :, u], start=False, stop=False)
                    last.then_inc(hist_used, 1)
            pe.matmul(deg_ps, zeros_b[:, :], zeros_b[:, 0:NB], start=False, stop=True).then_inc(deg_ready, 1)

            pairs = pe.alloc_register("pairs_pe")
            pe.wait_ge(bounds_ready, 1)
            for i in range(2):
                ps = gcn[i]
                pe.reg_mov(pairs, 0)
                with pe.Fori(0, ITERS) as it:
                    for s in range(RING):
                        g = it * RING + s
                        first, end = first_block(pe, g), end_block(pe, g)
                        pe.wait_ge(ps.gathered[s], (it + 1) * (16 * U))
                        pe.sem_inc(passed, 1)
                        with pe.Fori(first, end) as b:
                            pe.wait_ge(ps.added, pairs)
                            pe.reg_add(pairs, pairs, 1)
                            pe.wait_ge(ps.hot, pairs)
                            for u in range(U):
                                last = pe.matmul(pc[:, 0:TW], hot_lo[:, 0, :, u], gat_b[:, s, u * TW:(u + 1) * TW],
                                                 start=(u == 0), stop=(u == U - 1))
                            last.then_inc(ps.summed, 1)

            with pe.Fori(0, CHUNKS) as c:
                pe.wait_ge(ln2.ht, c)
                turn(lin2, c, lambda j: hch_in[:, j, :], HID)
                pe.wait_ge(lin2.ht, c + 1)
                pe.wait_ge(ln2.out, c)
                for j in range(CB):
                    last = pe.matmul(pb_f[:, j * F:(j + 1) * F], cht[0:HID, j, :], w2_sb[:, :], start=True, stop=True)
                last.then_inc(lin2.mm, 1)
                turn(ln2, c, lambda j: hch[:, j, :], P)
                pe.wait_ge(ln2.ht, c + 1)
                pe.wait_ge(lin2.out, c + 1)
                for j in range(CB):
                    last = pe.matmul(pb_f[:, j * F:(j + 1) * F], cht[:, j, :], wlin_sb[:, :], start=True, stop=True)
                last.then_inc(ln2.mm, 1)

            def turn_ea(g, it, s):
                pe.wait_ge(ea_loaded[s], (it + 1) * 16)
                pe.wait_ge(ea_out, g)
                for i in range(4):
                    last = pe.transpose(pd[:, i * P:(i + 1) * P], ea[:, s, i * P:(i + 1) * P], ident[:, :])
                last.then_inc(ea_turned, 1)

            def layer1(g):
                pe.wait_ge(ea_out, g + 1)
                pe.wait_ge(hid_act, g)
                for h in range(2):
                    half = slice(h * RBF, (h + 1) * RBF)
                    last = pe.matmul(pa[:, h, :], we1_sb[half, :], ea_t[half, :], start=True, stop=True)
                last.then_inc(hid_mm, 1)

            def layer2(g):
                pe.wait_ge(hid_act, g + 1)
                pe.wait_ge(msg_ready, g * 2)
                for h in range(2):
                    pe.matmul(pb[:, h, :], ones3[:, :], be2_parts[:, :, :].rearrange("p i f -> p (i f)"),
                              start=True, stop=False)
                    for i in range(4):
                        last = pe.matmul(pb[:, h, i * F:(i + 1) * F], act_t[:, h, i * P:(i + 1) * P], we2_sb[:, :],
                                         start=False, stop=(i == 3))
                last.then_inc(w_mm, 1)

            def lin_group(g, it, s, more=True):
                first, end = first_block(pe, g), end_block(pe, g)
                if more:
                    turn_ea(g + 1, it + (s + 1) // RING, (s + 1) % RING)
                layer2(g)
                if more:
                    layer1(g + 1)
                pe.wait_ge(msg_ready, g * 2 + 2)
                pe.sem_inc(passed, 1)
                with pe.Fori(first, end) as b:
                    pe.wait_ge(lin.added, pairs)
                    pe.reg_add(pairs, pairs, 1)
                    pe.wait_ge(lin.hot, pairs)
                    for h in range(2):
                        for i in range(4):
                            last = pe.matmul(pc[:, 0:F], hot_f[:, 2 * i + h, :], msg[:, h, i, :],
                                             start=(h == 0 and i == 0), stop=(h == 1 and i == 3))
                    last.then_inc(lin.summed, 1)

            pe.wait_ge(consts, 4)
            pe.reg_mov(pairs, 0)
            turn_ea(0, 0, 0)
            layer1(0)
            with pe.Fori(0, ITERS - 1) as it:
                for s in range(RING):
                    lin_group(it * RING + s, it, s)
            for s in range(RING):
                lin_group((ITERS - 1) * RING + s, ITERS - 1, s, more=(s < RING - 1))

            with pe.Fori(0, CHUNKS) as c:
                pe.wait_ge(down.out, c)
                turn(up, c, lambda j: c0[:, j, :], P)
                pe.wait_ge(up.ht, c + 1)
                rows = cht[:, :, :].rearrange("p b q -> p (b q)")
                pe.matmul(pb_f[:, 0:512], wn1_sb[:, :], rows[:, 0:512], start=True, stop=True)
                pe.matmul(pb_f[:, 512:CB * P], wn1_sb[:, :], rows[:, 512:CB * P], start=True, stop=True).then_inc(up.mm, 1)
                pe.wait_ge(up.out, c + 1)
                for j in range(CB):
                    last = pe.matmul(pa_f[:, j * F:(j + 1) * F], hch[:, j, :], wn2_sb[:, :], start=True, stop=True)
                last.then_inc(down.mm, 1)


_INS = ['x', 'src', 'dst', 'edge_attr_64', 'L0_gnn_W1', 'L0_gnn_b1', 'L0_gnn_W2', 'L0_gnn_b2', 'L1_gnn_We1', 'L1_gnn_be1',
        'L1_gnn_We2', 'L1_gnn_be2', 'L1_gnn_Wlin', 'L1_gnn_Wn1', 'L1_gnn_bn1', 'L1_gnn_Wn2', 'L1_gnn_bn2']


def kernel(**inputs):
    import numpy as _np
    import concourse.bacc as _bacc
    from concourse import mybir as _mybir
    from concourse.bass_utils import run_bass_kernel_spmd as _run

    nc = _bacc.Bacc("TRN2", target_bir_lowering=False, num_devices=1)
    arrays, args = {}, []
    for name in _INS:
        a = _np.ascontiguousarray(inputs[name])
        arrays[f"in_{name}_dram"] = a
        args.append(nc.dram_tensor(f"in_{name}_dram", a.shape, _mybir.dt.from_np(a.dtype), kind="ExternalInput").ap())
    args.append(nc.dram_tensor("out_dram", (N_NODES, F), _mybir.dt.float32, kind="ExternalOutput").ap())
    gnn_kernel(nc, *args)
    r = _run(nc, [arrays], core_ids=[0])
    return r.results[0]["out_dram"]
```

```python
import concourse.bass as bass
from concourse import mybir
from contextlib import ExitStack

fp32 = mybir.dt.float32
bf16 = mybir.dt.bfloat16
int32 = mybir.dt.int32
ALU = mybir.AluOpType
ACT = mybir.ActivationFunctionType
AX = mybir.AxisListType

P = 128
N_NODES, N_EDGES = 6250, 200000
F, HID, RBF = 128, 64, 64
NB = -(-N_NODES // P)
LAST_ROWS = N_NODES - (NB - 1) * P
W = 16
NW = NB * P // W
WB = P // W
WC = W * NB
CB = 7
CHUNKS = NB // CB
T = 2
UE = P * T
Q = 4
U = Q * T
GE = P * U
G = -(-N_EDGES // GE)
RING = 4
ITERS = G // RING
HALVES = -(-G // P)
FULL1 = N_EDGES // GE - P
TAIL = N_EDGES - (P + FULL1) * GE
G1 = G - P
UNITS = G * Q
NC = G * U
WP = NW // 4
FAR = 1024
EXACT = 256
PAD_DST = NB * P - 1
PARTS = 3
TW = PARTS * HID
EPS = 1e-5
assert NB == CHUNKS * CB and G == ITERS * RING and UE < TAIL < 2 * UE and TAIL % T == 0
assert NW == 4 * WP and WC // 2 <= 511 and FAR > UNITS
assert N_NODES <= PAD_DST


def gnn_kernel(nc, x, src, dst, edge_attr, W1, b1, W2, b2, We1, be1, We2, be2, Wlin, Wn1, bn1, Wn2, bn2, out):
    ctx = ExitStack()
    with ctx:
        def sb(name, shape, dt):
            return ctx.enter_context(nc.sbuf_tensor(name, shape, dt))

        def sem(name):
            return ctx.enter_context(nc.semaphore(name))

        gcn_table = [nc.dram_tensor(f"gcn_table{i}", (NB * P, TW), bf16, kind="Internal").ap() for i in range(2)]
        adjacency = nc.dram_tensor("adjacency", (NB, P, WB * WC), bf16, kind="Internal").ap()
        lin_table = nc.dram_tensor("lin_table", (NB * P, F), fp32, kind="Internal").ap()

        ident = sb("ident", [P, P], fp32)
        iota_f = sb("iota_f", [P, P], fp32)
        iota_u = sb("iota_u", [P, P, U], bf16)
        base_i = sb("base_i", [P, NB], int32)
        neg_base = sb("neg_base", [P, NB], fp32)
        eps_col = sb("eps_col", [P, 1], fp32)
        ones3 = sb("ones3", [PARTS, P], bf16)
        zeros_b = sb("zeros_b", [P, P], bf16)
        w1_sb = sb("w1_sb", [P, HID], fp32)
        w2_sb = sb("w2_sb", [HID, F], fp32)
        we1_sb = sb("we1_sb", [P, F], fp32)
        we2_sb = sb("we2_sb", [P, F], fp32)
        wlin_sb = sb("wlin_sb", [P, F], fp32)
        wn1_sb = sb("wn1_sb", [P, F], fp32)
        wn2_sb = sb("wn2_sb", [P, F], fp32)
        be1_col = sb("be1_col", [P, 1], fp32)
        bn1_col = sb("bn1_col", [P, 1], fp32)
        b1_all = sb("b1_all", [P, HID], fp32)
        b2_all = sb("b2_all", [P, F], fp32)
        bn2_all = sb("bn2_all", [P, F], fp32)
        be2_rows = sb("be2_rows", [PARTS, F], fp32)
        be2_hi = sb("be2_hi", [PARTS, F], bf16)
        be2_mid = sb("be2_mid", [PARTS, F], bf16)
        be2_lo = sb("be2_lo", [PARTS, F], bf16)
        be2_res = sb("be2_res", [PARTS, F], fp32)
        be2_parts = sb("be2_parts", [PARTS, 4, F], bf16)

        xr = sb("xr", [P, NB, F], fp32)
        agg = sb("agg", [P, NB * TW], fp32)
        agg_gcn = agg[:, :].rearrange("p (b c) -> p b c", b=NB)
        agg_lin = agg[:, 0:NB * F].rearrange("p (b c) -> p b c", b=NB)
        tmsg = sb("tmsg", [P, NB, HID], fp32)
        table_sb = sb("table_sb", [P, NB, TW], bf16)
        dinv = sb("dinv", [P, NB], fp32)
        deg_sb = sb("deg_sb", [P, NB], fp32)

        ADJ = 2 * WB * WC
        shared1 = sb("shared1", [P, 2 * ADJ // 4], fp32)
        shared2 = sb("shared2", [P, 2 * ADJ // 4], fp32)
        shared3 = sb("shared3", [P, 3 * NC], fp32)

        def part(mem, at, n, dt=fp32):
            v = mem[:, at:at + n]
            return v if dt is fp32 else v.bitcast(dt)

        def halves(v):
            return v.rearrange("p (k e) -> p k e", k=HALVES)

        RAW = HALVES * GE
        raw_d = halves(part(shared1, 0, RAW, int32))
        raw_s = halves(part(shared1, RAW, RAW, int32))
        raw_f = halves(part(shared1, 2 * RAW, RAW))
        dst_i = part(shared1, RAW, NC, int32)
        tmp_i = part(shared1, 0, NC, int32)
        pre = agg
        HOT = 2 * HALVES * Q * WP + UNITS + WC
        adj = [part(m, i * ADJ // 4, ADJ // 4, bf16) for m in (shared1, shared2) for i in range(2)]
        sq = part(shared2, 0, CB * F).rearrange("p (b f) -> p b f", f=F)
        dlo = part(shared2, CB * F, NC // 2, bf16)
        dhi = part(shared2, CB * F + NC // 2, NC // 2, bf16)
        idx_all = sb("idx_all", [P, NC], int32)
        dst_f = sb("dst_f", [P, NC], fp32)
        keys = [part(shared3, 0, NC), part(shared3, 2 * NC, NC)]
        src_lo = part(shared3, NC, NC // 2, bf16)
        um_i = sb("um_i", [P, 2, HALVES * Q], int32)
        um_f = sb("um_f", [P, 2, HALVES * Q], fp32)
        um_w = part(pre, 0, 2 * HALVES * Q * WP).rearrange("p (c w) -> p c w", w=WP)
        mm_i = sb("mm_i", [P, 2 * HALVES], int32)
        mm_f = sb("mm_f", [P, 2 * HALVES], fp32)
        unit_i = part(pre, 2 * HALVES * Q * WP, UNITS, int32)
        win_i = sb("win_i", [P, 4], int32)
        win_f = sb("win_f", [P, 4], fp32)
        win_lo = sb("win_lo", [P, 4], fp32)
        win_hi = sb("win_hi", [P, 4], fp32)
        windows = sb("windows", [1, 2, NW], int32)
        iota_i = part(pre, HOT + P * U + NB * U, P, int32)
        col_i = part(pre, 2 * HALVES * Q * WP + UNITS, WC, int32)
        col_h = sb("col_h", [P, WC], mybir.dt.float16)
        iota_t = sb("iota_t", [P, P, T], bf16)
        loop_lo = sb("loop_lo", [P, P, T], bf16)
        loop_col = sb("loop_col", [P, T, WC], bf16)
        counts = sb("counts", [P, NW], fp32)
        most = sb("most", [P, 1], fp32)
        over_f = sb("over_f", [1, 1], fp32)
        over_i = sb("over_i", [1, 1], int32)
        bounds = sb("bounds", [1, 2 * HALVES * P], int32)

        idx = sb("idx", [P, RING, U], int32)
        gat_w = part(shared2, 0, RING * U * F)
        gat = gat_w.rearrange("p (s u f) -> p s u f", s=RING, u=U)
        gat_b = gat_w.bitcast(bf16).rearrange("p (s c) -> p s c", s=RING)
        ea = part(shared2, RING * U * F, RING * U * RBF).rearrange("p (s c) -> p s c", s=RING)
        hch_in = part(shared2, CB * F, CB * HID).rearrange("p (b c) -> p b c", b=CB)
        hist_lo = part(pre, HOT, P * U, bf16).rearrange("p (s d u) -> p s d u", s=2, u=U)
        hist_hi = part(pre, HOT + P * U, NB * U, bf16).rearrange("p (s d u) -> p s d u", s=2, u=U)
        hot_b = part(shared3, 0, P * U // 2, bf16).rearrange("p (d u) -> p d u", u=U)
        dl_b = sb("dl_b", [P, U], bf16)
        dl_f = sb("dl_f", [P, U], fp32)
        hot_f = part(shared3, 0, U * P).rearrange("p (u d) -> p u d", u=U)
        ea_t = part(shared3, U * P, 4 * P)
        act_t = part(shared3, U * P + 4 * P, 8 * P).rearrange("p (h e) -> p h e", h=2)
        msg = part(shared3, U * P + 12 * P, 8 * F).rearrange("p (h i f) -> p h i f", h=2, i=4)

        c0 = sb("c0", [P, CB, F], fp32)
        c1 = sb("c1", [P, CB, F], fp32)
        hch = sb("hch", [P, CB, F], fp32)
        head_col = [m[:, :, :].rearrange("p b f -> p (b f)")[:, 0:T * WC // 2].bitcast(bf16).rearrange("p (t c) -> p t c", t=T)
                    for m in (c0, hch)]
        head_lo = [c1[:, i, :].bitcast(bf16).rearrange("p (d t) -> p d t", t=T) for i in range(2)]
        CHT = 3 * NC - CB * P
        assert CHT >= max(2 * NC, U * P + 12 * P + 8 * F)
        cht = part(shared3, CHT, CB * P).rearrange("p (b q) -> p b q", q=P)
        st = sb("st", [P, 4, CB], fp32)

        pa = ctx.enter_context(nc.psum_tensor("pa", [P, 2, 512], fp32))
        pb = ctx.enter_context(nc.psum_tensor("pb", [P, 2, 512], fp32))
        pc = ctx.enter_context(nc.psum_tensor("pc", [P, 512], fp32))
        pd = ctx.enter_context(nc.psum_tensor("pd", [P, 512], fp32))
        pa_f = pa[:, :, :].rearrange("p a b -> p (a b)")
        pb_f = pb[:, :, :].rearrange("p a b -> p (a b)")
        banks = [pa[:, 0, :], pa[:, 1, :], pb[:, 0, :], pb[:, 1, :]]
        deg_ps = pd[:, 0:NB]
        win_ps = [pa, pb]
        sums = [pc, pd]
        row_ps = pc[0:1, :]

        raw_set = sem("raw_set")
        raw_loaded = sem("raw_loaded")
        x_loaded = sem("x_loaded")
        w_loaded = sem("w_loaded")
        pool_consts = sem("pool_consts")
        consts = sem("consts")
        dve_done = sem("dve_done")
        act_done = sem("act_done")
        raw_fp = sem("raw_fp")
        turned = sem("turned")
        turned_out = sem("turned_out")
        mm_ready = sem("mm_ready")
        row_ready = sem("row_ready")
        bounds_ready = sem("bounds_ready")
        um_ready = sem("um_ready")
        um_rows = sem("um_rows")
        win_cols = sem("win_cols")
        win_rows = sem("win_rows")
        windows_ready = sem("windows_ready")
        key_ready = [sem(f"key_ready{i}") for i in range(2)]
        key_used = [sem(f"key_used{i}") for i in range(2)]
        head_hot = [sem(f"head_hot{i}") for i in range(2)]
        head_used = [sem(f"head_used{i}") for i in range(2)]
        tile_hot = [sem(f"tile_hot{t}") for t in range(T)]
        tile_used = [sem(f"tile_used{t}") for t in range(T)]
        win_ready = sem("win_ready")
        win_out = sem("win_out")
        adj_stored = [sem(f"adj_stored{i}") for i in range(2)]
        adj_loaded = [sem(f"adj_loaded{i}") for i in range(4)]
        sums_ready = [sem(f"sums_ready{i}") for i in range(2)]
        sums_out = [sem(f"sums_out{i}") for i in range(2)]
        most_ready = sem("most_ready")
        most_row = sem("most_row")
        over_ready = sem("over_ready")
        hist_hot = sem("hist_hot")
        hist_used = sem("hist_used")
        deg_ready = sem("deg_ready")

        class Node:
            def __init__(self, n):
                self.var = sem(f"{n}_var")
                self.std = sem(f"{n}_std")
                self.h = sem(f"{n}_h")
                self.turned = sem(f"{n}_turned")
                self.ht = sem(f"{n}_ht")
                self.mm = sem(f"{n}_mm")
                self.out = sem(f"{n}_out")
                self.stored = sem(f"{n}_stored")
        ln1, lin2, ln2 = Node("ln1"), Node("lin2"), Node("ln2")
        up, down = Node("up"), Node("down")
        split_ready = [sem(f"split_ready{i}") for i in range(2)]
        table_stored = [sem(f"table_stored{i}") for i in range(2)]
        out_stored = sem("out_stored")

        class Pass:
            def __init__(self, n):
                self.idx_ready = sem(f"{n}_idx_ready")
                self.gathered = [sem(f"{n}_gathered{s}") for s in range(RING)]
                self.rows_used = sem(f"{n}_rows_used")
                self.hot = sem(f"{n}_hot")
                self.summed = sem(f"{n}_summed")
                self.added = sem(f"{n}_added")
        gcn = [Pass("gcn0"), Pass("gcn1")]
        lin = Pass("lin")
        ea_loaded = [sem(f"ea_loaded{s}") for s in range(RING)]
        ea_clean = sem("ea_clean")
        ea_turned = sem("ea_turned")
        ea_out = sem("ea_out")
        hid_mm = sem("hid_mm")
        hid_act = sem("hid_act")
        w_mm = sem("w_mm")
        msg_ready = sem("msg_ready")

        passed = sem("passed")
        shared_free = sem("shared_free")

        N_W = 17
        N_POOL = 11
        block = ctx.enter_context(nc.Block())

        def window_spans(eng, regs, b):
            for m in range(2):
                eng.load(regs[m * WB:(m + 1) * WB], windows[0:1, m, bass.ds(b * WB, WB)])

        def group_blocks(eng, regs, g):
            eng.load(regs, bounds[0:1, bass.ds(g * 2, 2)])
            return eng.snap(regs[0], min_val=0, max_val=NB - 1), eng.snap(regs[1], min_val=1, max_val=NB)

        @block.sync
        def _(sp):
            sp.wait_ge(raw_set, 2)
            for raw, arr in ((raw_d, dst), (raw_s, src)):
                sp.dma_start(raw[:, 0, :], arr[0:P * GE].rearrange("(p e) -> p e", e=GE)).then_inc(raw_loaded, 16)
                sp.dma_start(raw[0:FULL1, 1, :],
                             arr[P * GE:(P + FULL1) * GE].rearrange("(p e) -> p e", e=GE)).then_inc(raw_loaded, 16)
                sp.dma_start(raw[FULL1:FULL1 + 1, 1, 0:TAIL],
                             arr[(P + FULL1) * GE:N_EDGES].rearrange("(p e) -> p e", p=1)).then_inc(raw_loaded, 16)
            sp.wait_ge(raw_set, 3)
            sp.dma_start(xr[:, 0:NB - 1, :], x[0:(NB - 1) * P, :].rearrange("(b p) f -> p b f", p=P)).then_inc(x_loaded, 16)
            sp.dma_start(xr[0:LAST_ROWS, NB - 1, :], x[(NB - 1) * P:N_NODES, :]).then_inc(x_loaded, 16)

            def row(v, n):
                return v.rearrange("(a n) -> a n", a=1).to_broadcast([n, v.shape[0]])
            loads = [(w1_sb[:, :], W1), (w2_sb[:, :], W2), (we1_sb[0:RBF, :], We1), (we1_sb[RBF:2 * RBF, :], We1),
                     (we2_sb[:, :], We2), (wlin_sb[:, :], Wlin), (wn1_sb[:, :], Wn1), (wn2_sb[:, :], Wn2),
                     (be1_col[:, :], be1.rearrange("(p a) -> p a", a=1)),
                     (bn1_col[:, :], bn1.rearrange("(p a) -> p a", a=1)),
                     (b1_all[:, :], row(b1, P)), (b2_all[:, :], row(b2, P)), (bn2_all[:, :], row(bn2, P)),
                     (be2_rows[:, :], row(be2, PARTS))]
            assert len(loads) == N_W - 3
            for to, of in loads:
                sp.dma_start(to, of).then_inc(w_loaded, 16)

            def store_adj(b, i):
                sp.wait_ge(win_out, (b + 1) * WB + 2)
                sp.dma_start(adjacency[bass.ds(b, 1), :, :].rearrange("a p c -> p (a c)"), adj[i]).then_inc(adj_stored[i], 16)
            store_adj(0, 0)
            with sp.Fori(0, NB // 2) as it:
                store_adj(it * 2 + 1, 1)
                store_adj(it * 2 + 2, 0)

            sp.wait_ge(over_ready, 1)
            over = sp.alloc_register("over_sp")
            sp.load(over, over_i[0:1, 0:1])

            def store_table(i):
                sp.wait_ge(split_ready[i], CHUNKS)
                sp.dma_start(gcn_table[i].rearrange("(b p) c -> p b c", p=P), table_sb[:, :, :]).then_inc(table_stored[i], 16)
            with sp.If_ne(over, 0):
                store_table(0)
                store_table(1)
            with sp.Else():
                def load_adj(b, i):
                    sp.dma_start(adj[i], adjacency[bass.ds(b, 1), :, :].rearrange("a p c -> p (a c)")).then_inc(adj_loaded[i], 16)
                sp.wait_ge(adj_stored[0], 16 * (NB // 2 + 1))
                sp.wait_ge(adj_stored[1], 16 * (NB // 2))
                sp.wait_ge(sums_out[0], NB + 2)
                for i in range(4):
                    load_adj(i, i)
                with sp.Fori(1, NB // 4) as it:
                    for i in range(4):
                        sp.wait_ge(sums_ready[1], it * 4 + (i - 3))
                        load_adj(it * 4 + i, i)
                sp.wait_ge(sums_ready[1], NB - 4)
                load_adj(NB - 1, 0)
                sp.wait_ge(sums_ready[1], NB)
            rows = lin_table.rearrange("(b p) c -> p b c", p=P)
            with sp.Fori(0, CHUNKS) as c:
                sp.wait_ge(ln2.out, c + 1)
                sp.dma_start(rows[:, bass.ds(c * CB, CB), :], c1[:, :, :]).then_inc(ln2.stored, 16)

            def load_ea(g, s):
                rows = edge_attr[bass.ds(g * GE, GE), :].rearrange("(q p t) f -> p q (t f)", q=Q, t=T)
                sp.dma_start(ea[:, s, :].rearrange("p (q c) -> p q c", q=Q), rows).then_inc(ea_loaded[s], 16)
            sp.wait_ge(ea_clean, 1)
            for s in range(RING):
                load_ea(s, s)
            with sp.Fori(1, ITERS - 1) as it:
                for s in range(RING):
                    sp.wait_ge(ea_turned, it * RING + (s - RING + 1))
                    load_ea(it * RING + s, s)
            for s in range(RING):
                g = (ITERS - 1) * RING + s
                sp.wait_ge(ea_turned, g - RING + 1)
                if g < G - 1:
                    load_ea(g, s)
                else:
                    sp.dma_start(ea[:, s, 0:T * RBF],
                                 edge_attr[g * GE:g * GE + UE, :].rearrange("(p t) f -> p (t f)", t=T)).then_inc(ea_loaded[s], 16)
                    sp.dma_start(ea[0:(TAIL - UE) // T, s, T * RBF:2 * T * RBF],
                                 edge_attr[g * GE + UE:N_EDGES, :].rearrange("(p t) f -> p (t f)", t=T)).then_inc(ea_loaded[s], 16)

            with sp.Fori(0, CHUNKS - 1) as c:
                sp.wait_ge(down.out, c + 1)
                sp.dma_start(out[bass.ds(c * (CB * P), CB * P), :].rearrange("(b p) f -> p b f", p=P),
                             c1[:, :, :]).then_inc(out_stored, 16)
            sp.wait_ge(down.out, CHUNKS)
            sp.dma_start(out[(NB - CB) * P:(NB - 1) * P, :].rearrange("(b p) f -> p b f", p=P),
                         c1[:, 0:CB - 1, :]).then_inc(out_stored, 16)
            sp.dma_start(out[(NB - 1) * P:N_NODES, :], c1[0:LAST_ROWS, CB - 1, :]).then_inc(out_stored, 16)
            sp.wait_ge(out_stored, 16 * (CHUNKS + 1))

        @block.gpsimd
        def _(pool):
            pool.memset(raw_d[:, 1, :], PAD_DST).then_inc(raw_set, 1)
            pool.iota(raw_s[:, 1, :], pattern=[[1, GE]], base=0, channel_multiplier=0).then_inc(raw_set, 1)
            pool.memset(xr[:, NB - 1, :], 0.0).then_inc(raw_set, 1)
            pool.iota(iota_i[:, :], pattern=[[1, P]], base=0, channel_multiplier=0).then_inc(pool_consts, 1)
            pool.iota(base_i[:, :], pattern=[[-P, NB]], base=0, channel_multiplier=0).then_inc(pool_consts, 1)
            pool.memset(ident[:, :], 0.0).then_inc(pool_consts, 1)
            pool.memset(ones3[:, :], 1.0).then_inc(pool_consts, 1)
            pool.memset(zeros_b[:, :], 0.0).then_inc(pool_consts, 1)
            pool.memset(eps_col[:, :], EPS).then_inc(pool_consts, 1)
            pool.iota(col_i[:, :], pattern=[[1, WC]], base=0, channel_multiplier=0).then_inc(pool_consts, 1)
            pool.iota(win_i[:, :], pattern=[[WP, 4]], base=0, channel_multiplier=1).then_inc(pool_consts, 1)
            pool.iota(unit_i[:, 0:Q * P], pattern=[[1, Q], [Q, P]], base=0, channel_multiplier=0).then_inc(pool_consts, 1)
            pool.iota(unit_i[:, Q * P:UNITS], pattern=[[1, Q], [Q, G1]], base=Q * P, channel_multiplier=0).then_inc(pool_consts, 1)
            pool.wait_ge(pool_consts, N_POOL - 1)
            pool.affine_select(out=ident[:, :], in_=ident[:, :], compare_op=ALU.not_equal, fill=1.0, base=0,
                               pattern=[[-1, P]], channel_multiplier=1).then_inc(pool_consts, 1)

            def gather(ps, table, dest, s):
                for j in range(U):
                    pool.indirect_dma_start(
                        out=dest(s, j), out_offset=None, in_=table,
                        in_offset=bass.IndirectOffsetOnAxis(ap=idx[:, s, j:j + 1], axis=0)).then_inc(ps.gathered[s], 16)

            def edge_pass(ps, table, dest, used, per):
                for s in range(RING):
                    pool.wait_ge(ps.idx_ready, s + 1)
                    gather(ps, table, dest, s)
                with pool.Fori(1, ITERS) as it:
                    for s in range(RING):
                        pool.wait_ge(ps.idx_ready, it * RING + (s + 1))
                        pool.wait_ge(used, (it * RING + (s - RING + 1)) * per)
                        pool.sem_inc(passed, 1)
                        gather(ps, table, dest, s)

            pool.wait_ge(shared_free, 1)
            pool.wait_ge(ln1.out, CHUNKS)
            pool.tensor_scalar(keys[1], keys[0], float(-P * NB), None, ALU.add).then_inc(key_ready[1], 1)
            pool.wait_ge(key_ready[1], 1)
            with pool.Fori(0, NB // 2) as it:
                for i in range(2):
                    pool.wait_ge(key_used[i], it + 1)
                    pool.sem_inc(passed, 1)
                    pool.tensor_scalar(keys[i], keys[i], float(-2 * P * NB), None, ALU.add).then_inc(key_ready[i], 1)

            pool.wait_ge(over_ready, 1)
            over = pool.alloc_register("over_pool")
            pool.load(over, over_i[0:1, 0:1])
            with pool.If_ne(over, 0):
                for i in range(2):
                    pool.wait_ge(table_stored[i], 16)
                    edge_pass(gcn[i], gcn_table[i], lambda s, j: gat_b[:, s, j * TW:(j + 1) * TW], gcn[i].rows_used, 1)
            pool.wait_ge(ln2.stored, 16 * CHUNKS)
            edge_pass(lin, lin_table, lambda s, j: gat[:, s, j, :], msg_ready, 2)

        @block.scalar
        def _(act):
            mine = act.alloc_register("act_steps")
            act.reg_mov(mine, 0)

            def step(ins):
                ins.then_inc(act_done, 1)
                act.reg_add(mine, mine, 1)
                act.wait_ge(act_done, mine)

            act.wait_ge(raw_loaded, 16 * 6)
            act.wait_ge(turned, 4)
            act.activation(raw_f[:, :, :], raw_s[:, :, :], ACT.Copy).then_inc(raw_fp, 1)

            def transposes_out(nd, c, n):
                act.wait_ge(nd.turned, c + 1)
                act.wait_ge(nd.mm, c)
                act.activation(cht[0:n, :, :], pa_f[0:n, 0:CB * P].rearrange("p (b q) -> p b q", q=P),
                               ACT.Copy).then_inc(nd.ht, 1)

            def std(nd, c):
                act.wait_ge(nd.var, c + 1)
                act.activation(st[:, 2, :], st[:, 1, :], ACT.Sqrt, bias=eps_col[:, :], scale=1.0 / F).then_inc(nd.std, 1)

            act.wait_ge(pool_consts, N_POOL)
            with act.Fori(0, CHUNKS) as c:
                std(ln1, c)
                transposes_out(ln1, c, P)
                act.wait_ge(ln1.mm, c + 1)
                act.activation(tmsg[:, bass.ds(c * CB, CB), :],
                               pb[:, 0, 0:CB * HID].rearrange("p (b q) -> p b q", q=HID), ACT.Copy).then_inc(ln1.out, 1)
            act.wait_ge(deg_ready, 1)
            act.activation(deg_sb[:, :], deg_ps, ACT.Sqrt, bias=1.0).then_inc(deg_ready, 1)

            def next_idx(ps, g, s):
                act.activation(idx[:, s, :], idx_all[:, bass.ds(g * U, U)], ACT.Copy).then_inc(ps.idx_ready, 1)

            def first_idx(ps):
                for s in range(RING):
                    next_idx(ps, s, s)

            def after_gather(ps, it, s):
                act.wait_ge(ps.gathered[s], (it + 1) * (16 * U))
                next_idx(ps, (it + 1) * RING + s, s)

            act.sem_inc(win_out, 2)
            act.sem_inc(sums_out[0], 2)
            act.sem_inc(sums_out[1], 2)

            def sums_copy(i, b, bank):
                act.wait_ge(sums_ready[i], b + 1)
                act.activation(agg_gcn[:, bass.ds(b, 1), :].rearrange("p a c -> p (a c)"), bank[:, 0:TW],
                               ACT.Copy).then_inc(sums_out[i], 1)

            def build_block(b, i, stored, first=False):
                if not first:
                    act.wait_ge(adj_stored[i], stored)
                for w in range(WB):
                    n = b * WB + w
                    act.wait_ge(win_ready, n + 1)
                    act.activation(adj[i][:, w * WC:(w + 1) * WC].rearrange("p (h c) -> p h c", h=2),
                                   win_ps[w % 2][:, :, 0:WC // 2], ACT.Copy,
                                   accum_out=counts[:, bass.ds(n, 1)]).then_inc(win_out, 1)
                if not first:
                    sums_copy(0, b - 1, sums[1 - i])
            act.wait_ge(shared_free, 1)
            build_block(0, 0, 0, first=True)
            with act.Fori(0, NB // 2) as it:
                build_block(it * 2 + 1, 1, it * 16)
                build_block(it * 2 + 2, 0, it * 16 + 16)
            sums_copy(0, NB - 1, sums[0])

            act.wait_ge(over_ready, 1)
            over = act.alloc_register("over_act")
            act.load(over, over_i[0:1, 0:1])

            def gather_idx(i):
                first_idx(gcn[i])
                with act.Fori(0, ITERS - 1) as it:
                    for s in range(RING):
                        after_gather(gcn[i], it, s)
                for s in range(RING):
                    act.wait_ge(gcn[i].gathered[s], ITERS * 16 * U)
            with act.If_ne(over, 0):
                gather_idx(0)
                gather_idx(1)
            with act.Else():
                act.wait_ge(split_ready[1], CHUNKS)
                with act.Fori(0, NB // 4) as it:
                    for i in range(4):
                        sums_copy(1, it * 4 + i, sums[i % 2])
                sums_copy(1, NB - 1, sums[0])

            with act.Fori(0, CHUNKS) as c:
                transposes_out(lin2, c, HID)
                std(ln2, c)
                transposes_out(ln2, c, P)
                act.wait_ge(ln2.mm, c + 1)
                act.wait_ge(ln2.stored, c * 16)
                act.activation(c1[:, :, :], pb_f[:, 0:CB * F].rearrange("p (b q) -> p b q", q=F),
                               ACT.Copy).then_inc(ln2.out, 1)

            def edge_act(g):
                act.wait_ge(ea_turned, g + 1)
                act.wait_ge(hid_mm, g * 2)
                act.activation(ea_t[:, :], pd[:, :], ACT.Copy).then_inc(ea_out, 1)
                for h in range(2):
                    act.wait_ge(hid_mm, g * 2 + (h + 1))
                    if not isinstance(g, int) or g > 0:
                        act.wait_ge(w_mm, g * 2 + (h - 1))
                    act.activation(act_t[:, h, :], pa[:, h, :], ACT.Silu, bias=be1_col[:, :]).then_inc(hid_act, 1)

            first_idx(lin)
            edge_act(0)
            with act.Fori(0, ITERS - 1) as it:
                for s in range(RING):
                    edge_act(it * RING + (s + 1))
                    after_gather(lin, it, s)
            for s in range(RING - 1):
                edge_act((ITERS - 1) * RING + s + 1)

            with act.Fori(0, CHUNKS) as c:
                transposes_out(up, c, P)
                act.wait_ge(up.mm, c + 1)
                act.wait_ge(down.mm, c)
                act.activation(hch[:, :, :], pb_f[:, 0:CB * P].rearrange("p (b q) -> p b q", q=P), ACT.Silu,
                               bias=bn1_col[:, :]).then_inc(up.out, 1)

        @block.vector
        def _(dve):
            mine = dve.alloc_register("dve_steps")
            dve.reg_mov(mine, 0)

            def step(ins):
                ins.then_inc(dve_done, 1)
                dve.reg_add(mine, mine, 1)
                dve.wait_ge(dve_done, mine)

            def bc(ap, n):
                return ap.rearrange("p (b a) -> p b a", a=1).to_broadcast([P, ap.shape[1], n])

            def lanes(t, g, n):
                return t[:, bass.ds(g * U, U)].rearrange("p (a u) -> p a u", a=1).to_broadcast([P, n, U])

            dve.wait_ge(pool_consts, N_POOL - 1)
            step(dve.tensor_copy(iota_f[:, :], iota_i[:, :]))
            step(dve.tensor_copy(iota_u[:, :, :], bc(iota_i[:, :], U)))
            step(dve.tensor_copy(iota_t[:, :, :], bc(iota_i[:, :], T)))
            step(dve.tensor_copy(neg_base[:, :], base_i[:, :]))
            step(dve.tensor_copy(col_h[:, :], col_i[:, :]))
            step(dve.tensor_copy(win_f[:, :], win_i[:, :]))

            dve.wait_ge(raw_loaded, 16 * 6)
            dve.tensor_copy(raw_f[:, :, :], raw_d[:, :, :]).then_inc(raw_fp, 1)
            by_unit = raw_d.rearrange("p k (q e) -> p (k q) e", q=Q)
            for m, op in enumerate((ALU.min, ALU.max)):
                step(dve.tensor_reduce(um_i[:, m, :], by_unit, AX.X, op))
                step(dve.tensor_reduce(mm_i[:, m * HALVES:(m + 1) * HALVES],
                                       um_i[:, m, :].rearrange("p (k q) -> p k q", q=Q), AX.X, op))
            step(dve.tensor_scalar(um_i[:, :, :], um_i[:, :, :], 4, None, ALU.arith_shift_right))
            step(dve.tensor_copy(um_f[:, :, :], um_i[:, :, :]))
            dve.tensor_copy(um_w[:, :, :], bc(um_f[:, :, :].rearrange("p m c -> p (m c)"), WP)).then_inc(um_ready, 1)
            step(dve.tensor_scalar(mm_i[:, :], mm_i[:, :], 7, None, ALU.arith_shift_right))
            step(dve.tensor_copy(mm_f[:, :], mm_i[:, :]))
            dve.tensor_scalar(mm_f[:, HALVES:2 * HALVES], mm_f[:, HALVES:2 * HALVES], 1.0, None, ALU.add).then_inc(mm_ready, 1)
            dve.wait_ge(row_ready, 1)
            dve.tensor_copy(bounds[:, :].rearrange("a (g m) -> a m g", m=2), row_ps.rearrange("a (m g) -> a m g", m=2)).then_inc(bounds_ready, 1)

            def turned_copy(n, m, to):
                k, r = m // 2, m % 2
                gs = P if k == 0 else G1
                view = to[:, k * GE:k * GE + gs * U].rearrange("p (g j) -> p j g", j=U)[:, 4 * r:4 * r + 4, :]
                dve.wait_ge(turned, n + 1)
                dve.tensor_copy(view, banks[m].rearrange("p (j g) -> p j g", g=P)[:, :, 0:gs]).then_inc(turned_out, 1)
            for m in range(4):
                turned_copy(m, m, dst_f[:, :])
            for m in range(4):
                turned_copy(4 + m, m, idx_all[:, :])
            dve.wait_ge(turned_out, 8)
            step(dve.tensor_copy(dst_i, dst_f[:, :]))
            step(dve.tensor_scalar(tmp_i, dst_i, P - 1, None, ALU.bitwise_and))
            step(dve.tensor_copy(dlo, tmp_i))
            step(dve.tensor_scalar(tmp_i, dst_i, 7, None, ALU.arith_shift_right))
            step(dve.tensor_copy(dhi, tmp_i))
            step(dve.tensor_scalar(tmp_i, idx_all[:, :], P - 1, None, ALU.bitwise_and))
            step(dve.tensor_copy(src_lo, tmp_i))
            step(dve.tensor_scalar(tmp_i, idx_all[:, :], 7, None, ALU.arith_shift_right))
            dve.scalar_tensor_tensor(keys[0], dst_f[:, :], float(NB), tmp_i, ALU.mult, ALU.add).then_inc(shared_free, 1)
            dve.sem_inc(key_ready[0], 1)
            dve.wait_ge(shared_free, 1)

            dve.wait_ge(um_rows, 1)
            some = c0[0:WP, :, :].rearrange("p b f -> p (b f)")[:, 0:UNITS]
            which = c1[0:WP, :, :].rearrange("p b f -> p (b f)")[:, 0:UNITS]
            for i in range(4):
                step(dve.tensor_scalar(some, pa_f[0:WP, 0:UNITS], win_f[0:WP, i:i + 1], None, ALU.is_le))
                step(dve.scalar_tensor_tensor(some, pb_f[0:WP, 0:UNITS], win_f[0:WP, i:i + 1], some, ALU.is_ge, ALU.mult))
                step(dve.scalar_tensor_tensor(which, unit_i[0:WP, :], float(-FAR), some, ALU.add, ALU.mult))
                step(dve.tensor_reduce(win_lo[0:WP, i:i + 1], which, AX.X, ALU.min))
                step(dve.scalar_tensor_tensor(which, unit_i[0:WP, :], 1.0, some, ALU.add, ALU.mult))
                step(dve.tensor_reduce(win_hi[0:WP, i:i + 1], which, AX.X, ALU.max))
            step(dve.tensor_scalar(win_lo[0:WP, :], win_lo[0:WP, :], float(FAR + 2), float(UNITS), ALU.add, ALU.min))
            dve.tensor_tensor(win_hi[0:WP, :], win_hi[0:WP, :], win_lo[0:WP, :], ALU.max).then_inc(win_cols, 1)
            dve.wait_ge(win_rows, 1)
            dve.tensor_copy(windows[:, :, :], pa[0:1, :, 0:NW]).then_inc(windows_ready, 1)

            dve.wait_ge(w_loaded, 16 * (N_W - 3))
            dve.wait_ge(pool_consts, N_POOL)
            step(dve.tensor_copy(be2_hi[:, :], be2_rows[:, :]))
            step(dve.tensor_tensor(be2_res[:, :], be2_rows[:, :], be2_hi[:, :], ALU.subtract))
            step(dve.tensor_copy(be2_mid[:, :], be2_res[:, :]))
            step(dve.tensor_tensor(be2_lo[:, :], be2_res[:, :], be2_mid[:, :], ALU.subtract))
            step(dve.tensor_scalar(be2_res[:, :], be2_hi[:, :], ident[0:PARTS, 0:1], None, ALU.mult))
            step(dve.scalar_tensor_tensor(be2_res[:, :], be2_mid[:, :], ident[0:PARTS, 1:2], be2_res[:, :], ALU.mult, ALU.add))
            step(dve.scalar_tensor_tensor(be2_res[:, :], be2_lo[:, :], ident[0:PARTS, 2:3], be2_res[:, :], ALU.mult, ALU.add))
            for i in range(4):
                dve.tensor_copy(be2_parts[:, i, :], be2_res[:, :]).then_inc(consts, 1)

            def layernorm_relu(nd, c, rows):
                step(dve.tensor_reduce(st[:, 0, :], rows, AX.X, ALU.add))
                step(dve.tensor_scalar(st[:, 0, :], st[:, 0, :], -1.0 / F, None, ALU.mult))
                step(dve.tensor_tensor(c0[:, :, :], rows, bc(st[:, 0, :], F), ALU.add))
                step(dve.tensor_tensor(sq, c0[:, :, :], c0[:, :, :], ALU.mult))
                dve.tensor_reduce(st[:, 1, :], sq, AX.X, ALU.add).then_inc(nd.var, 1)
                dve.wait_ge(nd.std, c + 1)
                step(dve.reciprocal(st[:, 3, :], st[:, 2, :]))
                dve.wait_ge(nd.turned, c)
                dve.scalar_tensor_tensor(hch[:, :, :], c0[:, :, :], 0.0, bc(st[:, 3, :], F), ALU.max, ALU.mult).then_inc(nd.h, 1)
                dve.wait_ge(nd.h, c + 1)
            dve.wait_ge(x_loaded, 32)
            with dve.Fori(0, CHUNKS) as c:
                layernorm_relu(ln1, c, xr[:, bass.ds(c * CB, CB), :])

            with dve.Fori(0, ITERS * RING // 2) as it:
                for s in range(2):
                    g = it * 2 + s
                    dve.wait_ge(hist_used, it * 2 + s)
                    dve.tensor_tensor(hist_lo[:, s, :, :], iota_u[:, :, :], lanes(dlo, g, P), ALU.is_equal)\
                       .then_inc(hist_hot, 1)
                    dve.tensor_tensor(hist_hi[:, s, :, :], iota_u[:, 0:NB, :], lanes(dhi, g, NB), ALU.is_equal)\
                       .then_inc(hist_hot, 1)
            dve.wait_ge(deg_ready, 2)
            step(dve.reciprocal(dinv[:, :], deg_sb[:, :]))
            dve.sem_inc(passed, 1)

            def split_out(i, c, tm):
                t = table_sb[:, bass.ds(c * CB, CB), :]
                dve.sem_inc(passed, 1)
                step(dve.tensor_copy(t[:, :, 0:HID], tm))
                dve.sem_inc(passed, 1)
                step(dve.tensor_tensor(c0[:, :, 0:HID], tm, t[:, :, 0:HID], ALU.subtract))
                dve.sem_inc(passed, 1)
                step(dve.tensor_copy(t[:, :, HID:2 * HID], c0[:, :, 0:HID]))
                dve.tensor_tensor(t[:, :, 2 * HID:3 * HID], c0[:, :, 0:HID], t[:, :, HID:2 * HID],
                                  ALU.subtract).then_inc(split_ready[i], 1)
                dve.wait_ge(split_ready[i], c + 1)

            dve.wait_ge(ln1.out, CHUNKS)
            with dve.Fori(0, CHUNKS) as c:
                tm = tmsg[:, bass.ds(c * CB, CB), :]
                step(dve.tensor_tensor(tm, tm, bc(dinv[:, bass.ds(c * CB, CB)], HID), ALU.mult))
                split_out(0, c, tm)

            pairs = dve.alloc_register("pairs_dve")
            span = [dve.alloc_register(f"span_dve{i}") for i in range(2)]
            dve.wait_ge(bounds_ready, 1)

            def gcn_pass(ps):
                dve.reg_mov(pairs, 0)
                with dve.Fori(0, G) as g:
                    first, end = group_blocks(dve, span, g)
                    with dve.Fori(first, end) as b:
                        step(dve.tensor_scalar(dl_b[:, :], dst_f[:, bass.ds(g * U, U)], neg_base[:, bass.ds(b, 1)], None, ALU.add))
                        dve.tensor_tensor(hot_b, iota_u[:, :, :],
                                          dl_b[:, :].rearrange("p (a u) -> p a u", a=1).to_broadcast([P, P, U]),
                                          ALU.is_equal).then_inc(ps.hot, 1)
                        dve.reg_add(pairs, pairs, 1)
                        dve.wait_ge(ps.summed, pairs)
                        a = agg_gcn[:, bass.ds(b, 1), :].rearrange("p a c -> p (a c)")
                        dve.tensor_tensor(a, a, pc[:, 0:TW], ALU.add).then_inc(ps.added, 1)
                    dve.sem_inc(ps.rows_used, 1)
                dve.wait_ge(ps.added, pairs)
                dve.sem_inc(passed, 1)

            units = dve.alloc_register("units_dve")
            dve.reg_mov(units, 1)
            for t in range(T):
                dve.sem_inc(tile_hot[t], 1)
            ranges = [dve.alloc_register(f"range_dve{i}") for i in range(2 * WB)]
            dve.wait_ge(windows_ready, 1)

            def columns(to, i, tile, w):
                return dve.tensor_scalar(to, col_h[:, :], keys[i][:, bass.ds(tile, 1)], float(-WC * w), ALU.subtract, ALU.is_equal)

            def sources(to, tile):
                return dve.tensor_tensor(to[:, :, :], iota_t[:, :, :],
                                         src_lo[:, bass.ds(tile, T)].rearrange("p (a t) -> p a t", a=1).to_broadcast([P, P, T]),
                                         ALU.is_equal)

            def build_block(b, i, k, first=False):
                window_spans(dve, ranges, b)
                dve.wait_ge(key_ready[i], k + 1)
                dve.sem_inc(passed, 1)
                for w in range(WB):
                    third = dve.snap(ranges[w], min_val=2, max_val=UNITS)
                    for j in range(2):
                        tile = third * T - (2 - j) * T
                        dve.wait_ge(head_used[j], b * WB + (w + 1))
                        sources(head_lo[j], tile)
                        for t in range(T):
                            columns(head_col[j][:, t, :], i, tile + t, w).then_inc(head_hot[j], 1)
                    if w == 0 and not first:
                        dve.wait_ge(head_hot[1], b * (WB * T))
                        dve.sem_inc(passed, 1)
                        dve.wait_ge(tile_hot[T - 1], units)
                        dve.sem_inc(key_used[1 - i], 1)
                    with dve.If_lt(ranges[w], ranges[WB + w]):
                        with dve.Fori(third, dve.snap(ranges[WB + w], min_val=3, max_val=UNITS)) as u:
                            dve.reg_add(units, units, 1)
                            dve.wait_ge(tile_used[0], units)
                            columns(loop_col[:, 0, :], i, u * T, w)
                            dve.wait_ge(tile_used[1], units)
                            sources(loop_lo, u * T).then_inc(tile_hot[0], 1)
                            columns(loop_col[:, 1, :], i, u * T + 1, w).then_inc(tile_hot[1], 1)

            build_block(0, 0, 0, first=True)
            with dve.Fori(0, NB // 2) as it:
                build_block(it * 2 + 1, 1, it)
                build_block(it * 2 + 2, 0, it + 1)

            dve.wait_ge(key_ready[1], NB // 2 + 1)
            dve.wait_ge(win_out, NW + 2)
            dve.tensor_reduce(most[:, :], counts[:, :], AX.X, ALU.max).then_inc(most_ready, 1)
            dve.wait_ge(most_row, 1)
            step(dve.tensor_reduce(over_f[:, :], pa[0:1, 0, 0:P], AX.X, ALU.max))
            dve.tensor_scalar(over_i[:, :], over_f[:, :], float(EXACT), None, ALU.is_ge).then_inc(over_ready, 1)
            dve.wait_ge(over_ready, 1)
            over = dve.alloc_register("over_dve")
            dve.load(over, over_i[0:1, 0:1])

            dve.wait_ge(sums_out[0], NB + 2)
            with dve.If_ne(over, 0):
                step(dve.memset(agg[:, :], 0.0))
                dve.sem_inc(passed, 1)
                gcn_pass(gcn[0])
                dve.wait_ge(table_stored[0], 16)

            def gcn_sum(c):
                blocks = bass.ds(c * CB, CB)
                a = agg_gcn[:, blocks, :]
                tm = tmsg[:, blocks, :]
                step(dve.tensor_tensor(c0[:, :, 0:HID], a[:, :, 0:HID], a[:, :, HID:2 * HID], ALU.add))
                step(dve.tensor_tensor(c0[:, :, 0:HID], c0[:, :, 0:HID], a[:, :, 2 * HID:3 * HID], ALU.add))
                step(dve.tensor_tensor(c0[:, :, 0:HID], c0[:, :, 0:HID], tm, ALU.add))
                step(dve.tensor_tensor(c0[:, :, 0:HID], c0[:, :, 0:HID], bc(dinv[:, blocks], HID), ALU.mult))
                return tm, a

            def all_rows(ap):
                return ap.rearrange("p (a n) -> p a n", a=1).to_broadcast([P, CB, ap.shape[1]])

            with dve.Fori(0, CHUNKS) as c:
                tm, a = gcn_sum(c)
                step(dve.tensor_tensor(c0[:, :, 0:HID], c0[:, :, 0:HID], all_rows(b1_all[:, :]), ALU.add))
                step(dve.scalar_tensor_tensor(tm, c0[:, :, 0:HID], 0.0, bc(dinv[:, bass.ds(c * CB, CB)], HID), ALU.max, ALU.mult))
                split_out(1, c, tm)
            with dve.If_ne(over, 0):
                step(dve.memset(agg[:, :], 0.0))
                dve.sem_inc(passed, 1)
                gcn_pass(gcn[1])
            with dve.Else():
                dve.wait_ge(sums_out[1], NB + 2)
            dve.sem_inc(ea_clean, 1)

            with dve.Fori(0, CHUNKS) as c:
                rows = xr[:, bass.ds(c * CB, CB), :]
                tm, a = gcn_sum(c)
                dve.wait_ge(lin2.turned, c)
                dve.tensor_copy(hch_in[:, :, :], c0[:, :, 0:HID]).then_inc(lin2.h, 1)
                step(dve.tensor_tensor(rows, rows, all_rows(b2_all[:, :]), ALU.add))
                dve.wait_ge(lin2.mm, c + 1)
                step(dve.tensor_tensor(rows, rows, pb_f[:, 0:CB * F].rearrange("p (b q) -> p b q", q=F), ALU.add))
                dve.sem_inc(lin2.out, 1)
                layernorm_relu(ln2, c, rows)
                step(dve.tensor_tensor(rows, rows, hch[:, :, :], ALU.add))
                step(dve.tensor_tensor(rows, rows, all_rows(bn2_all[:, :]), ALU.add))
            step(dve.memset(agg[:, 0:NB * F], 0.0))
            dve.sem_inc(passed, 1)

            dve.reg_mov(pairs, 0)

            def messages(g, turns, s):
                rows = gat[:, s, :, :].rearrange("p (i h) f -> p h i f", h=2)
                dve.wait_ge(lin.gathered[s], turns * (16 * U))
                dve.sem_inc(passed, 1)
                for h in range(2):
                    dve.wait_ge(w_mm, g * 2 + (h + 1))
                    dve.tensor_tensor(msg[:, h, :, :], pb[:, h, :].rearrange("p (i f) -> p i f", f=F),
                                      rows[:, h, :, :], ALU.mult).then_inc(msg_ready, 1)

            def group_sums(g):
                first, end = group_blocks(dve, span, g)
                with dve.Fori(first, end) as b:
                    step(dve.tensor_scalar(dl_f[:, :], dst_f[:, bass.ds(g * U, U)], neg_base[:, bass.ds(b, 1)], None, ALU.add))
                    dve.tensor_tensor(hot_f[:, :, :], iota_f[:, :].rearrange("p (a d) -> p a d", a=1).to_broadcast([P, U, P]),
                                      bc(dl_f[:, :], P), ALU.is_equal).then_inc(lin.hot, 1)
                    dve.reg_add(pairs, pairs, 1)
                    dve.wait_ge(lin.summed, pairs)
                    a = agg_lin[:, bass.ds(b, 1), :].rearrange("p a c -> p (a c)")
                    dve.tensor_tensor(a, a, pc[:, 0:F], ALU.add).then_inc(lin.added, 1)

            messages(0, 1, 0)
            with dve.Fori(0, ITERS - 1) as it:
                for s in range(1, RING + 1):
                    g = it * RING + s
                    group_sums(g - 1)
                    messages(g, it + (s // RING + 1), s % RING)
            for s in range(1, RING):
                g = (ITERS - 1) * RING + s
                group_sums(g - 1)
                messages(g, ITERS, s)
            group_sums(G - 1)
            dve.wait_ge(lin.added, pairs)
            dve.sem_inc(passed, 1)

            with dve.Fori(0, CHUNKS) as c:
                blocks = bass.ds(c * CB, CB)
                dve.wait_ge(up.turned, c)
                dve.sem_inc(passed, 1)
                dve.tensor_copy(c0[:, :, :], agg_lin[:, blocks, :]).then_inc(up.h, 1)
                dve.wait_ge(down.mm, c + 1)
                dve.wait_ge(out_stored, c * 16)
                dve.tensor_tensor(c1[:, :, :], xr[:, blocks, :], pa_f[:, 0:CB * F].rearrange("p (b q) -> p b q", q=F),
                                  ALU.add).then_inc(down.out, 1)

        @block.tensor
        def _(pe):
            pe.wait_ge(pool_consts, N_POOL)
            for a in range(2):
                pe.wait_ge(raw_fp, a + 1)
                for k in range(HALVES):
                    for r in range(2):
                        n = 2 * k + r
                        if a == 1:
                            pe.wait_ge(turned_out, n + 1)
                        cols = raw_f[:, k, :]
                        for j in range(4):
                            q, t = divmod(4 * r + j, T)
                            edges = cols[:, q * UE:(q + 1) * UE].rearrange("p (e t) -> p t e", t=T)[:, t, :]
                            last = pe.transpose(banks[n][:, j * P:(j + 1) * P], edges, ident[:, :])
                        last.then_inc(turned, 1)
                if a == 0:
                    pe.wait_ge(mm_ready, 1)
                    for i in range(2 * HALVES):
                        last = pe.matmul(pc[0:1, i * P:(i + 1) * P], mm_f[:, i:i + 1], ident[:, :], start=True, stop=True)
                    last.then_inc(row_ready, 1)

            pe.wait_ge(um_ready, 1)
            pe.wait_ge(turned_out, 8)
            for m, to in enumerate((pa_f, pb_f)):
                at = 0
                for k in range(HALVES):
                    gs = P if k == 0 else G1
                    for q in range(Q):
                        last = pe.matmul(to[0:WP, at:at + gs], um_w[:, (m * HALVES + k) * Q + q, :], ident[:, 0:gs],
                                         start=True, stop=True)
                        at += gs
            last.then_inc(um_rows, 1)
            pe.wait_ge(win_cols, 1)
            for m, cols in enumerate((win_lo, win_hi)):
                for i in range(4):
                    last = pe.matmul(pa[0:1, m, i * WP:(i + 1) * WP], cols[0:WP, i:i + 1], ident[0:WP, 0:WP],
                                     start=True, stop=True)
            last.then_inc(win_rows, 1)

            def turn(nd, c, rows, n):
                pe.wait_ge(nd.h, c + 1)
                pe.wait_ge(nd.ht, c)
                pe.sem_inc(passed, 1)
                for j in range(CB):
                    last = pe.transpose(pa_f[0:n, j * P:(j + 1) * P], rows(j), ident[:, :])
                last.then_inc(nd.turned, 1)

            pe.wait_ge(w_loaded, 16 * (N_W - 3))
            pe.wait_ge(windows_ready, 1)
            with pe.Fori(0, CHUNKS) as c:
                turn(ln1, c, lambda j: hch[:, j, :], P)
                pe.wait_ge(ln1.ht, c + 1)
                pe.wait_ge(ln1.out, c)
                for j in range(CB):
                    last = pe.matmul(pb[:, 0, j * HID:(j + 1) * HID], cht[:, j, :], w1_sb[:, :], start=True, stop=True)
                last.then_inc(ln1.mm, 1)

            pe.matmul(deg_ps, zeros_b[:, :], zeros_b[:, 0:NB], start=True, stop=False).then_inc(hist_used, 1)
            with pe.Fori(0, ITERS * RING // 2) as it:
                for s in range(2):
                    pe.wait_ge(hist_hot, (it * 2 + s) * 2 + 2)
                    for u in range(U):
                        last = pe.matmul(deg_ps, hist_lo[:, s, :, u], hist_hi[:, s, :, u], start=False, stop=False)
                    last.then_inc(hist_used, 1)
            pe.matmul(deg_ps, zeros_b[:, :], zeros_b[:, 0:NB], start=False, stop=True).then_inc(deg_ready, 1)

            units = pe.alloc_register("units_pe")
            pe.reg_mov(units, 1)
            ranges = [pe.alloc_register(f"range_pe{i}") for i in range(2 * WB)]
            for t in range(T):
                pe.sem_inc(tile_used[t], 2)
                pe.sem_inc(head_used[t], 1)

            def edge_sum(ps, first):
                for h in range(2):
                    last = pe.matmul(ps[:, h, 511:512], zeros_b[:, :], zeros_b[:, 0:1], start=first, stop=not first)
                return last

            def convolve(i, b, block, bank, blocks=range(NB)):
                if blocks[0] == 0:
                    pe.wait_ge(sums_out[i], b + 1)
                    pe.sem_inc(passed, 1)
                by_source = block.rearrange("p (d h) -> p h d", h=NB)
                for h in blocks:
                    last = pe.matmul(bank[:, 0:TW], by_source[:, h, :], table_sb[:, h, :], start=(h == 0), stop=(h == NB - 1))
                if blocks[-1] == NB - 1:
                    last.then_inc(sums_ready[i], 1)

            def tile_counts(ps, lo, col, t):
                for h in range(2):
                    last = pe.matmul(ps[:, h, 0:WC // 2], lo[:, :, t], col[:, t, h * WC // 2:(h + 1) * WC // 2],
                                     start=False, stop=False)
                return last

            def build_block(b, i, first=False):
                window_spans(pe, ranges, b)
                for w in range(WB):
                    ps = win_ps[w % 2]
                    pe.wait_ge(win_out, b * WB + w + 1)
                    pe.sem_inc(passed, 1)
                    edge_sum(ps, True)
                    for j in range(2):
                        for t in range(T):
                            pe.wait_ge(head_hot[j], (b * WB + w) * T + (t + 1))
                            last = tile_counts(ps, head_lo[j], head_col[j], t)
                        last.then_inc(head_used[j], 1)
                    with pe.If_lt(ranges[w], ranges[WB + w]):
                        with pe.Fori(ranges[w], ranges[WB + w]):
                            pe.reg_add(units, units, 1)
                            for t in range(T):
                                pe.wait_ge(tile_hot[t], units)
                                tile_counts(ps, loop_lo, loop_col, t).then_inc(tile_used[t], 1)
                    edge_sum(ps, False).then_inc(win_ready, 1)
                    if w > 0 and not first:
                        convolve(0, b - 1, adj[1 - i], sums[1 - i], range((w - 1) * NB // (WB - 1), w * NB // (WB - 1)))

            pe.wait_ge(ln1.out, CHUNKS)
            pe.wait_ge(deg_ready, 2)
            build_block(0, 0, first=True)
            pe.wait_ge(split_ready[0], CHUNKS)
            with pe.Fori(0, NB // 2) as it:
                build_block(it * 2 + 1, 1)
                build_block(it * 2 + 2, 0)
            pe.wait_ge(win_out, NW + 2)
            convolve(0, NB - 1, adj[0], sums[0])
            pe.wait_ge(most_ready, 1)
            pe.transpose(pa[0:1, 0, 0:P], most[:, :], ident[:, :]).then_inc(most_row, 1)

            pairs = pe.alloc_register("pairs_pe")
            span = [pe.alloc_register(f"span_pe{i}") for i in range(2)]
            pe.wait_ge(bounds_ready, 1)
            pe.wait_ge(over_ready, 1)
            over = pe.alloc_register("over_pe")
            pe.load(over, over_i[0:1, 0:1])

            def gcn_pass(ps):
                pe.reg_mov(pairs, 0)
                with pe.Fori(0, ITERS) as it:
                    for s in range(RING):
                        g = it * RING + s
                        first, end = group_blocks(pe, span, g)
                        pe.wait_ge(ps.gathered[s], (it + 1) * (16 * U))
                        pe.sem_inc(passed, 1)
                        with pe.Fori(first, end) as b:
                            pe.wait_ge(ps.added, pairs)
                            pe.reg_add(pairs, pairs, 1)
                            pe.wait_ge(ps.hot, pairs)
                            for u in range(U):
                                last = pe.matmul(pc[:, 0:TW], hot_b[:, :, u], gat_b[:, s, u * TW:(u + 1) * TW],
                                                 start=(u == 0), stop=(u == U - 1))
                            last.then_inc(ps.summed, 1)
            with pe.If_ne(over, 0):
                gcn_pass(gcn[0])
                gcn_pass(gcn[1])
            with pe.Else():
                pe.wait_ge(split_ready[1], CHUNKS)
                with pe.Fori(0, NB // 4) as it:
                    for i in range(4):
                        pe.wait_ge(adj_loaded[i], it * 16 + 16)
                        convolve(1, it * 4 + i, adj[i], sums[i % 2])
                pe.wait_ge(adj_loaded[0], (NB // 4 + 1) * 16)
                convolve(1, NB - 1, adj[0], sums[0])

            with pe.Fori(0, CHUNKS) as c:
                pe.wait_ge(ln2.ht, c)
                turn(lin2, c, lambda j: hch_in[:, j, :], HID)
                pe.wait_ge(lin2.ht, c + 1)
                pe.wait_ge(ln2.out, c)
                for j in range(CB):
                    last = pe.matmul(pb_f[:, j * F:(j + 1) * F], cht[0:HID, j, :], w2_sb[:, :], start=True, stop=True)
                last.then_inc(lin2.mm, 1)
                turn(ln2, c, lambda j: hch[:, j, :], P)
                pe.wait_ge(ln2.ht, c + 1)
                pe.wait_ge(lin2.out, c + 1)
                for j in range(CB):
                    last = pe.matmul(pb_f[:, j * F:(j + 1) * F], cht[:, j, :], wlin_sb[:, :], start=True, stop=True)
                last.then_inc(ln2.mm, 1)

            def turn_ea(g, turns, s):
                pe.wait_ge(ea_loaded[s], turns * 16)
                pe.wait_ge(ea_out, g)
                for i in range(4):
                    last = pe.transpose(pd[:, i * P:(i + 1) * P], ea[:, s, i * P:(i + 1) * P], ident[:, :])
                last.then_inc(ea_turned, 1)

            def layer1(g):
                pe.wait_ge(ea_out, g + 1)
                for h in range(2):
                    half = slice(h * RBF, (h + 1) * RBF)
                    pe.matmul(pa[:, h, :], we1_sb[half, :], ea_t[half, :], start=True, stop=True).then_inc(hid_mm, 1)

            def layer2(g):
                for h in range(2):
                    if not isinstance(g, int) or g > 0:
                        pe.wait_ge(msg_ready, g * 2 + (h - 1))
                        pe.sem_inc(passed, 1)
                    pe.matmul(pb[:, h, :], ones3[:, :], be2_parts[:, :, :].rearrange("p i f -> p (i f)"),
                              start=True, stop=False)
                    pe.wait_ge(hid_act, g * 2 + (h + 1))
                    for i in range(4):
                        last = pe.matmul(pb[:, h, i * F:(i + 1) * F], act_t[:, h, i * P:(i + 1) * P], we2_sb[:, :],
                                         start=False, stop=(i == 3))
                    last.then_inc(w_mm, 1)

            def group_sums(g):
                first, end = group_blocks(pe, span, g)
                pe.wait_ge(msg_ready, g * 2 + 2)
                pe.sem_inc(passed, 1)
                with pe.Fori(first, end) as b:
                    pe.wait_ge(lin.added, pairs)
                    pe.reg_add(pairs, pairs, 1)
                    pe.wait_ge(lin.hot, pairs)
                    for h in range(2):
                        for i in range(4):
                            last = pe.matmul(pc[:, 0:F], hot_f[:, 2 * i + h, :], msg[:, h, i, :],
                                             start=(h == 0 and i == 0), stop=(h == 1 and i == 3))
                    last.then_inc(lin.summed, 1)

            pe.wait_ge(consts, 4)
            pe.reg_mov(pairs, 0)
            turn_ea(0, 1, 0)
            layer1(0)
            turn_ea(1, 1, 1)
            layer2(0)
            layer1(1)
            with pe.Fori(0, ITERS - 1) as it:
                for s in range(1, RING + 1):
                    g = it * RING + s
                    turn_ea(g + 1, it + ((s + 1) // RING + 1), (s + 1) % RING)
                    layer2(g)
                    group_sums(g - 1)
                    layer1(g + 1)
            for g in range((ITERS - 1) * RING + 1, G):
                if g < G - 1:
                    turn_ea(g + 1, ITERS + (1 if g + 1 == G - 1 else 0), (g + 1) % RING)
                layer2(g)
                group_sums(g - 1)
                if g < G - 1:
                    layer1(g + 1)
            group_sums(G - 1)

            with pe.Fori(0, CHUNKS) as c:
                pe.wait_ge(down.out, c)
                turn(up, c, lambda j: c0[:, j, :], P)
                pe.wait_ge(up.ht, c + 1)
                rows = cht[:, :, :].rearrange("p b q -> p (b q)")
                pe.matmul(pb_f[:, 0:512], wn1_sb[:, :], rows[:, 0:512], start=True, stop=True)
                pe.matmul(pb_f[:, 512:CB * P], wn1_sb[:, :], rows[:, 512:CB * P], start=True, stop=True).then_inc(up.mm, 1)
                pe.wait_ge(up.out, c + 1)
                for j in range(CB):
                    last = pe.matmul(pa_f[:, j * F:(j + 1) * F], hch[:, j, :], wn2_sb[:, :], start=True, stop=True)
                last.then_inc(down.mm, 1)


_INS = ['x', 'src', 'dst', 'edge_attr_64', 'L0_gnn_W1', 'L0_gnn_b1', 'L0_gnn_W2', 'L0_gnn_b2', 'L1_gnn_We1', 'L1_gnn_be1',
        'L1_gnn_We2', 'L1_gnn_be2', 'L1_gnn_Wlin', 'L1_gnn_Wn1', 'L1_gnn_bn1', 'L1_gnn_Wn2', 'L1_gnn_bn2']


def kernel(**inputs):
    import numpy as _np
    import concourse.bacc as _bacc
    from concourse import mybir as _mybir
    from concourse.bass_utils import run_bass_kernel_spmd as _run

    nc = _bacc.Bacc("TRN2", target_bir_lowering=False, num_devices=1)
    arrays, args = {}, []
    for name in _INS:
        a = _np.ascontiguousarray(inputs[name])
        arrays[f"in_{name}_dram"] = a
        args.append(nc.dram_tensor(f"in_{name}_dram", a.shape, _mybir.dt.from_np(a.dtype), kind="ExternalInput").ap())
    args.append(nc.dram_tensor("out_dram", (N_NODES, F), _mybir.dt.float32, kind="ExternalOutput").ap())
    gnn_kernel(nc, *args)
    r = _run(nc, [arrays], core_ids=[0])
    return r.results[0]["out_dram"]
```

```python
import concourse.bass as bass
from concourse import mybir
from contextlib import ExitStack

fp32 = mybir.dt.float32
bf16 = mybir.dt.bfloat16
int32 = mybir.dt.int32
ALU = mybir.AluOpType
ACT = mybir.ActivationFunctionType
AX = mybir.AxisListType

P = 128
N_NODES, N_EDGES = 6250, 200000
F, HID, RBF = 128, 64, 64
NB = -(-N_NODES // P)
LAST_ROWS = N_NODES - (NB - 1) * P
W = 16
NW = NB * P // W
WB = P // W
WC = W * NB
CB = 7
CHUNKS = NB // CB
RB = 4
BATCHES = NB // RB
T = 2
UE = P * T
Q = 4
U = Q * T
GE = P * U
G = -(-N_EDGES // GE)
RING = 4
ITERS = G // RING
HALVES = -(-G // P)
FULL1 = N_EDGES // GE - P
TAIL = N_EDGES - (P + FULL1) * GE
G1 = G - P
UNITS = G * Q
NC = G * U
WP = NW // 4
FAR = 1024
EXACT = 256
PAD_DST = NB * P - 1
PARTS = 3
TW = PARTS * HID
EPS = 1e-5
assert NB == CHUNKS * CB and NB == BATCHES * RB + 1 and G == ITERS * RING and UE < TAIL < 2 * UE and TAIL % T == 0
assert NW == 4 * WP and WC // 2 <= 511 and FAR > UNITS
assert N_NODES <= PAD_DST


def gnn_kernel(nc, x, src, dst, edge_attr, W1, b1, W2, b2, We1, be1, We2, be2, Wlin, Wn1, bn1, Wn2, bn2, out):
    ctx = ExitStack()
    with ctx:
        def sb(name, shape, dt):
            return ctx.enter_context(nc.sbuf_tensor(name, shape, dt))

        def sem(name):
            return ctx.enter_context(nc.semaphore(name))

        gcn_table = [nc.dram_tensor(f"gcn_table{i}", (NB * P, TW), bf16, kind="Internal").ap() for i in range(2)]
        adjacency = nc.dram_tensor("adjacency", (NB, P, WB * WC), bf16, kind="Internal").ap()
        lin_table = nc.dram_tensor("lin_table", (NB * P, F), fp32, kind="Internal").ap()

        ident = sb("ident", [P, P], fp32)
        iota_f = sb("iota_f", [P, P], fp32)
        iota_u = sb("iota_u", [P, P, U], bf16)
        base_i = sb("base_i", [P, NB], int32)
        neg_base = sb("neg_base", [P, NB], fp32)
        eps_col = sb("eps_col", [P, 1], fp32)
        ones3 = sb("ones3", [PARTS, P], bf16)
        zeros_b = sb("zeros_b", [P, P], bf16)
        w1_sb = sb("w1_sb", [P, HID], fp32)
        w2_sb = sb("w2_sb", [HID, F], fp32)
        we1_sb = sb("we1_sb", [P, F], fp32)
        we2_sb = sb("we2_sb", [P, F], fp32)
        wlin_sb = sb("wlin_sb", [P, F], fp32)
        wn1_sb = sb("wn1_sb", [P, F], fp32)
        wn2_sb = sb("wn2_sb", [P, F], fp32)
        be1_col = sb("be1_col", [P, 1], fp32)
        bn1_col = sb("bn1_col", [P, 1], fp32)
        b1_all = sb("b1_all", [P, HID], fp32)
        b2_all = sb("b2_all", [P, F], fp32)
        bn2_all = sb("bn2_all", [P, F], fp32)
        be2_rows = sb("be2_rows", [PARTS, F], fp32)
        be2_hi = sb("be2_hi", [PARTS, F], bf16)
        be2_mid = sb("be2_mid", [PARTS, F], bf16)
        be2_lo = sb("be2_lo", [PARTS, F], bf16)
        be2_res = sb("be2_res", [PARTS, F], fp32)
        be2_parts = sb("be2_parts", [PARTS, 4, F], bf16)

        xr = sb("xr", [P, NB, F], fp32)
        agg = sb("agg", [P, NB * TW], fp32)
        agg_gcn = agg[:, :].rearrange("p (b c) -> p b c", b=NB)
        agg_lin = agg[:, 0:NB * F].rearrange("p (b c) -> p b c", b=NB)
        tmsg = sb("tmsg", [P, NB, HID], fp32)
        table_sb = sb("table_sb", [P, NB, TW], bf16)
        dinv = sb("dinv", [P, NB], fp32)
        neg_mean = sb("neg_mean", [P, NB], fp32)
        std1 = sb("std1", [P, NB], fp32)
        deg_sb = sb("deg_sb", [P, NB], fp32)

        ADJ = 2 * WB * WC
        shared1 = sb("shared1", [P, 2 * ADJ // 4], fp32)
        shared2 = sb("shared2", [P, 2 * ADJ // 4], fp32)
        shared3 = sb("shared3", [P, 3 * NC], fp32)

        def part(mem, at, n, dt=fp32):
            v = mem[:, at:at + n]
            return v if dt is fp32 else v.bitcast(dt)

        def halves(v):
            return v.rearrange("p (k e) -> p k e", k=HALVES)

        RAW = HALVES * GE
        raw_d = halves(part(shared1, 0, RAW, int32))
        raw_s = halves(part(shared1, RAW, RAW, int32))
        raw_f = halves(part(shared1, 2 * RAW, RAW))
        dst_i = part(shared1, RAW, NC, int32)
        tmp_i = part(shared1, 0, NC, int32)
        pre = agg
        HOT = 2 * HALVES * Q * WP + UNITS + WC
        adj = [part(m, i * ADJ // 4, ADJ // 4, bf16) for m in (shared1, shared2) for i in range(2)]
        sq = part(shared3, 0, RB * F).rearrange("p (b f) -> p b f", f=F)
        hch_in = part(shared3, RB * F, RB * HID).rearrange("p (b c) -> p b c", b=RB)
        bt = [part(shared3, RB * (F + HID + i * P), RB * P).rearrange("p (b q) -> p b q", q=P) for i in range(2)]
        dlo = part(shared2, CB * F, NC // 2, bf16)
        dhi = part(shared2, CB * F + NC // 2, NC // 2, bf16)
        idx_all = sb("idx_all", [P, NC], int32)
        dst_f = sb("dst_f", [P, NC], fp32)
        keys = [part(shared3, 0, NC), part(shared3, 2 * NC, NC)]
        src_lo = part(shared3, NC, NC // 2, bf16)
        um_i = sb("um_i", [P, 2, HALVES * Q], int32)
        um_f = sb("um_f", [P, 2, HALVES * Q], fp32)
        um_w = part(pre, 0, 2 * HALVES * Q * WP).rearrange("p (c w) -> p c w", w=WP)
        mm_i = sb("mm_i", [P, 2 * HALVES], int32)
        mm_f = sb("mm_f", [P, 2 * HALVES], fp32)
        unit_i = part(pre, 2 * HALVES * Q * WP, UNITS, int32)
        win_i = sb("win_i", [P, 4], int32)
        win_f = sb("win_f", [P, 4], fp32)
        win_lo = sb("win_lo", [P, 4], fp32)
        win_hi = sb("win_hi", [P, 4], fp32)
        windows = sb("windows", [1, NB + 1, 2, WB], int32)
        iota_i = part(pre, HOT + P * U + NB * U, P, int32)
        LATE = CHUNKS - 2
        unused = [part(pre, HOT + P * U + NB * U + P, LATE * CB * F).rearrange("p (b f) -> p b f", f=F),
                  part(shared2, CB * F + NC, (CHUNKS - LATE) * CB * F).rearrange("p (b f) -> p b f", f=F)]
        col_i = part(pre, 2 * HALVES * Q * WP + UNITS, WC, int32)
        col_h = sb("col_h", [P, WC], mybir.dt.float16)
        iota_t = sb("iota_t", [P, P, T], bf16)
        loop_lo = sb("loop_lo", [P, P, T], bf16)
        loop_col = sb("loop_col", [P, T, WC], bf16)
        counts = sb("counts", [P, NW], fp32)
        most = sb("most", [P, 1], fp32)
        over_f = sb("over_f", [1, 1], fp32)
        over_i = sb("over_i", [1, 1], int32)
        bounds = sb("bounds", [1, 2 * HALVES * P], int32)

        idx = sb("idx", [P, RING, U], int32)
        gat_w = part(shared2, 0, RING * U * F)
        gat = gat_w.rearrange("p (s u f) -> p s u f", s=RING, u=U)
        gat_b = gat_w.bitcast(bf16).rearrange("p (s c) -> p s c", s=RING)
        ea = part(shared2, RING * U * F, RING * U * RBF).rearrange("p (s c) -> p s c", s=RING)
        hist_lo = part(pre, HOT, P * U, bf16).rearrange("p (s d u) -> p s d u", s=2, u=U)
        hist_hi = part(pre, HOT + P * U, NB * U, bf16).rearrange("p (s d u) -> p s d u", s=2, u=U)
        hot_b = part(shared3, 0, P * U // 2, bf16).rearrange("p (d u) -> p d u", u=U)
        dl_b = sb("dl_b", [P, U], bf16)
        dl_f = sb("dl_f", [P, U], fp32)
        hot_f = part(shared3, 0, U * P).rearrange("p (u d) -> p u d", u=U)
        ea_t = part(shared3, U * P, 4 * P)
        act_t = part(shared3, U * P + 4 * P, 8 * P).rearrange("p (h e) -> p h e", h=2)
        msg = part(shared3, U * P + 12 * P, 8 * F).rearrange("p (h i f) -> p h i f", h=2, i=4)

        c0 = sb("c0", [P, CB, F], fp32)
        c1 = sb("c1", [P, CB, F], fp32)
        hch = sb("hch", [P, CB, F], fp32)
        hid = [c0, hch]
        head_col = [m[:, :, :].rearrange("p b f -> p (b f)")[:, 0:T * WC // 2].bitcast(bf16).rearrange("p (t c) -> p t c", t=T)
                    for m in (c0, hch)]
        head_lo = [c1[:, 2 * i:2 * i + 2, :].rearrange("p b f -> p (b f)").bitcast(bf16).rearrange("p (d t) -> p d t", t=2 * T)
                   for i in range(2)]
        CHT = 3 * NC - CB * P
        assert CHT >= max(2 * NC, U * P + 12 * P + 8 * F)
        cht = part(shared3, CHT, CB * P).rearrange("p (b q) -> p b q", q=P)
        st = sb("st", [P, 4, CB], fp32)

        pa = ctx.enter_context(nc.psum_tensor("pa", [P, 2, 512], fp32))
        pb = ctx.enter_context(nc.psum_tensor("pb", [P, 2, 512], fp32))
        pc = ctx.enter_context(nc.psum_tensor("pc", [P, 512], fp32))
        pd = ctx.enter_context(nc.psum_tensor("pd", [P, 512], fp32))
        pa_f = pa[:, :, :].rearrange("p a b -> p (a b)")
        pb_f = pb[:, :, :].rearrange("p a b -> p (a b)")
        banks = [pa[:, 0, :], pa[:, 1, :], pb[:, 0, :], pb[:, 1, :]]
        deg_ps = pd[:, 0:NB]
        win_ps = [pa, pb]
        sums = [pc, pd]
        mlp_out = [pc, pd]
        row_ps = pc[0:1, :]

        raw_set = sem("raw_set")
        raw_loaded = sem("raw_loaded")
        x_loaded = sem("x_loaded")
        w_loaded = sem("w_loaded")
        pool_consts = sem("pool_consts")
        consts = sem("consts")
        dve_done = sem("dve_done")
        act_done = sem("act_done")
        raw_fp = sem("raw_fp")
        turned = sem("turned")
        turned_out = sem("turned_out")
        mm_ready = sem("mm_ready")
        row_ready = sem("row_ready")
        bounds_ready = sem("bounds_ready")
        um_ready = sem("um_ready")
        um_rows = sem("um_rows")
        win_cols = sem("win_cols")
        win_rows = sem("win_rows")
        windows_ready = sem("windows_ready")
        key_ready = [sem(f"key_ready{i}") for i in range(2)]
        key_used = [sem(f"key_used{i}") for i in range(2)]
        head_hot = [sem(f"head_hot{i}") for i in range(2)]
        head_used = [sem(f"head_used{i}") for i in range(2)]
        tile_hot = [sem(f"tile_hot{t}") for t in range(T)]
        tile_used = [sem(f"tile_used{t}") for t in range(T)]
        win_ready = sem("win_ready")
        win_out = sem("win_out")
        adj_stored = [sem(f"adj_stored{i}") for i in range(2)]
        adj_loaded = [sem(f"adj_loaded{i}") for i in range(4)]
        sums_ready = [sem(f"sums_ready{i}") for i in range(2)]
        sums_out = [sem(f"sums_out{i}") for i in range(2)]
        most_ready = sem("most_ready")
        most_row = sem("most_row")
        over_ready = sem("over_ready")
        hist_hot = sem("hist_hot")
        hist_used = sem("hist_used")
        deg_ready = sem("deg_ready")

        class Node:
            def __init__(self, n):
                self.var = sem(f"{n}_var")
                self.std = sem(f"{n}_std")
                self.h = sem(f"{n}_h")
                self.turned = sem(f"{n}_turned")
                self.ht = sem(f"{n}_ht")
                self.mm = sem(f"{n}_mm")
                self.out = sem(f"{n}_out")
                self.stored = sem(f"{n}_stored")
        ln1, lin2, ln2 = Node("ln1"), Node("lin2"), Node("ln2")
        up, down = Node("up"), Node("down")
        tm_ready = sem("tm_ready")
        hi_ready = sem("hi_ready")
        rest_ready = sem("rest_ready")
        mid_ready = sem("mid_ready")
        split_ready = [sem(f"split_ready{i}") for i in range(2)]
        table_stored = [sem(f"table_stored{i}") for i in range(2)]
        out_stored = sem("out_stored")
        rows_free = sem("rows_free")

        class Pass:
            def __init__(self, n):
                self.idx_ready = sem(f"{n}_idx_ready")
                self.gathered = [sem(f"{n}_gathered{s}") for s in range(RING)]
                self.rows_used = sem(f"{n}_rows_used")
                self.hot = sem(f"{n}_hot")
                self.summed = sem(f"{n}_summed")
                self.added = sem(f"{n}_added")
        gcn = [Pass("gcn0"), Pass("gcn1")]
        lin = Pass("lin")
        ea_loaded = [sem(f"ea_loaded{s}") for s in range(RING)]
        ea_clean = sem("ea_clean")
        ea_turned = sem("ea_turned")
        ea_out = sem("ea_out")
        hid_mm = sem("hid_mm")
        hid_act = sem("hid_act")
        w_mm = sem("w_mm")
        msg_ready = sem("msg_ready")

        passed = sem("passed")
        shared_free = sem("shared_free")

        N_W = 17
        N_POOL = 11
        block = ctx.enter_context(nc.Block())

        TABLE_HALVES = [slice(0, (NB + 1) // 2), slice((NB + 1) // 2, NB)]

        def part_of(i):
            return slice(i * HID, (i + 1) * HID)

        def window_spans(eng, regs, b):
            eng.load(regs, windows[0:1, bass.ds(b, 1), :, :].rearrange("a b m w -> a (b m w)"))

        def group_blocks(eng, regs, g):
            eng.load(regs, bounds[0:1, bass.ds(g * 2, 2)])
            return eng.snap(regs[0], min_val=0, max_val=NB - 1), eng.snap(regs[1], min_val=1, max_val=NB)

        @block.sync
        def _(sp):
            sp.wait_ge(raw_set, 2)
            for raw, arr in ((raw_d, dst), (raw_s, src)):
                sp.dma_start(raw[:, 0, :], arr[0:P * GE].rearrange("(p e) -> p e", e=GE)).then_inc(raw_loaded, 16)
                sp.dma_start(raw[0:FULL1, 1, :],
                             arr[P * GE:(P + FULL1) * GE].rearrange("(p e) -> p e", e=GE)).then_inc(raw_loaded, 16)
                sp.dma_start(raw[FULL1:FULL1 + 1, 1, 0:TAIL],
                             arr[(P + FULL1) * GE:N_EDGES].rearrange("(p e) -> p e", p=1)).then_inc(raw_loaded, 16)
            sp.wait_ge(raw_set, 3)
            sp.dma_start(xr[:, 0:NB - 1, :], x[0:(NB - 1) * P, :].rearrange("(b p) f -> p b f", p=P)).then_inc(x_loaded, 16)
            sp.dma_start(xr[0:LAST_ROWS, NB - 1, :], x[(NB - 1) * P:N_NODES, :]).then_inc(x_loaded, 16)

            def row(v, n):
                return v.rearrange("(a n) -> a n", a=1).to_broadcast([n, v.shape[0]])
            loads = [(w1_sb[:, :], W1), (w2_sb[:, :], W2), (we1_sb[0:RBF, :], We1), (we1_sb[RBF:2 * RBF, :], We1),
                     (we2_sb[:, :], We2), (wlin_sb[:, :], Wlin), (wn1_sb[:, :], Wn1), (wn2_sb[:, :], Wn2),
                     (be1_col[:, :], be1.rearrange("(p a) -> p a", a=1)),
                     (bn1_col[:, :], bn1.rearrange("(p a) -> p a", a=1)),
                     (b1_all[:, :], row(b1, P)), (b2_all[:, :], row(b2, P)), (bn2_all[:, :], row(bn2, P)),
                     (be2_rows[:, :], row(be2, PARTS))]
            assert len(loads) == N_W - 3
            for to, of in loads:
                sp.dma_start(to, of).then_inc(w_loaded, 16)

            def store_adj(b, i):
                sp.wait_ge(win_out, (b + 1) * WB + 2)
                sp.dma_start(adjacency[bass.ds(b, 1), :, :].rearrange("a p c -> p (a c)"), adj[i]).then_inc(adj_stored[i], 16)
            store_adj(0, 0)
            with sp.Fori(0, NB // 2) as it:
                store_adj(it * 2 + 1, 1)
                store_adj(it * 2 + 2, 0)

            sp.wait_ge(over_ready, 1)
            over = sp.alloc_register("over_sp")
            sp.load(over, over_i[0:1, 0:1])

            def store_table(i):
                sp.wait_ge(split_ready[i], 2)
                sp.dma_start(gcn_table[i].rearrange("(b p) c -> p b c", p=P), table_sb[:, :, :]).then_inc(table_stored[i], 16)
            with sp.If_ne(over, 0):
                store_table(0)
                store_table(1)
            with sp.Else():
                def load_adj(b, i):
                    sp.dma_start(adj[i], adjacency[bass.ds(b, 1), :, :].rearrange("a p c -> p (a c)")).then_inc(adj_loaded[i], 16)
                sp.wait_ge(adj_stored[0], 16 * (NB // 2 + 1) + 1)
                sp.wait_ge(adj_stored[1], 16 * (NB // 2) + 1)
                sp.wait_ge(sums_out[0], NB + 2)
                for i in range(4):
                    load_adj(i, i)
                with sp.Fori(1, BATCHES) as it:
                    for i in range(4):
                        sp.wait_ge(sums_ready[1], it * 4 + (i - 3))
                        load_adj(it * 4 + i, i)
                sp.wait_ge(sums_ready[1], NB - 4)
                load_adj(NB - 1, 0)
                sp.wait_ge(sums_ready[1], NB)
            def load_ea(g, s):
                rows = edge_attr[bass.ds(g * GE, GE), :].rearrange("(q p t) f -> p q (t f)", q=Q, t=T)
                sp.dma_start(ea[:, s, :].rearrange("p (q c) -> p q c", q=Q), rows).then_inc(ea_loaded[s], 16)
            sp.wait_ge(ea_clean, 1)
            for s in range(RING):
                load_ea(s, s)
            with sp.Fori(1, ITERS - 1) as it:
                for s in range(RING):
                    sp.wait_ge(ea_turned, it * RING + (s - RING + 1))
                    load_ea(it * RING + s, s)
            for s in range(RING):
                g = (ITERS - 1) * RING + s
                sp.wait_ge(ea_turned, g - RING + 1)
                if g < G - 1:
                    load_ea(g, s)
                else:
                    sp.dma_start(ea[:, s, 0:T * RBF],
                                 edge_attr[g * GE:g * GE + UE, :].rearrange("(p t) f -> p (t f)", t=T)).then_inc(ea_loaded[s], 16)
                    sp.dma_start(ea[0:(TAIL - UE) // T, s, T * RBF:2 * T * RBF],
                                 edge_attr[g * GE + UE:N_EDGES, :].rearrange("(p t) f -> p (t f)", t=T)).then_inc(ea_loaded[s], 16)

            for k in range(BATCHES):
                sp.wait_ge(down.out, k + 1)
                sp.dma_start(out[k * RB * P:(k + 1) * RB * P, :].rearrange("(b p) f -> p b f", p=P),
                             xr[:, k * RB:(k + 1) * RB, :]).then_inc(out_stored, 16)
            sp.wait_ge(down.out, BATCHES + 1)
            sp.dma_start(out[(NB - 1) * P:N_NODES, :], xr[0:LAST_ROWS, NB - 1, :]).then_inc(out_stored, 16)
            sp.wait_ge(out_stored, 16 * (BATCHES + 1))

        @block.gpsimd
        def _(pool):
            pool.memset(raw_d[:, 1, :], PAD_DST).then_inc(raw_set, 1)
            pool.iota(raw_s[:, 1, :], pattern=[[1, GE]], base=0, channel_multiplier=0).then_inc(raw_set, 1)
            pool.memset(xr[:, NB - 1, :], 0.0).then_inc(raw_set, 1)
            pool.iota(iota_i[:, :], pattern=[[1, P]], base=0, channel_multiplier=0).then_inc(pool_consts, 1)
            pool.iota(base_i[:, :], pattern=[[-P, NB]], base=0, channel_multiplier=0).then_inc(pool_consts, 1)
            pool.memset(ident[:, :], 0.0).then_inc(pool_consts, 1)
            pool.memset(ones3[:, :], 1.0).then_inc(pool_consts, 1)
            pool.memset(zeros_b[:, :], 0.0).then_inc(pool_consts, 1)
            pool.memset(eps_col[:, :], EPS).then_inc(pool_consts, 1)
            pool.iota(col_i[:, :], pattern=[[1, WC]], base=0, channel_multiplier=0).then_inc(pool_consts, 1)
            pool.iota(win_i[:, :], pattern=[[WP, 4]], base=0, channel_multiplier=1).then_inc(pool_consts, 1)
            pool.iota(unit_i[:, 0:Q * P], pattern=[[1, Q], [Q, P]], base=0, channel_multiplier=0).then_inc(pool_consts, 1)
            pool.iota(unit_i[:, Q * P:UNITS], pattern=[[1, Q], [Q, G1]], base=Q * P, channel_multiplier=0).then_inc(pool_consts, 1)
            pool.wait_ge(pool_consts, N_POOL - 1)
            pool.affine_select(out=ident[:, :], in_=ident[:, :], compare_op=ALU.not_equal, fill=1.0, base=0,
                               pattern=[[-1, P]], channel_multiplier=1).then_inc(pool_consts, 1)

            def gather(ps, table, dest, s):
                for j in range(U):
                    pool.indirect_dma_start(
                        out=dest(s, j), out_offset=None, in_=table,
                        in_offset=bass.IndirectOffsetOnAxis(ap=idx[:, s, j:j + 1], axis=0)).then_inc(ps.gathered[s], 16)

            def edge_pass(ps, table, dest, used, per):
                for s in range(RING):
                    pool.wait_ge(ps.idx_ready, s + 1)
                    gather(ps, table, dest, s)
                with pool.Fori(1, ITERS) as it:
                    for s in range(RING):
                        pool.wait_ge(ps.idx_ready, it * RING + (s + 1))
                        pool.wait_ge(used, (it * RING + (s - RING + 1)) * per)
                        pool.sem_inc(passed, 1)
                        gather(ps, table, dest, s)

            pool.wait_ge(over_ready, 1)
            over = pool.alloc_register("over_pool")
            pool.load(over, over_i[0:1, 0:1])
            with pool.If_ne(over, 0):
                for i in range(2):
                    pool.wait_ge(table_stored[i], 16)
                    edge_pass(gcn[i], gcn_table[i], lambda s, j: gat_b[:, s, j * TW:(j + 1) * TW], gcn[i].rows_used, 1)
            rows = lin_table.rearrange("(b p) c -> p b c", p=P)
            pool.sem_inc(rows_free, 1)
            with pool.Fori(0, BATCHES) as k:
                pool.wait_ge(ln2.out, k + 1)
                pool.sem_inc(passed, 1)
                pool.dma_start(rows[:, bass.ds(k * RB, RB), :], c1[:, 0:RB, :]).then_inc(ln2.stored, 16)
                pool.wait_ge(ln2.stored, k * 16 + 16)
                pool.sem_inc(rows_free, 1)
            pool.wait_ge(ln2.out, BATCHES + 1)
            pool.dma_start(rows[:, NB - 1:NB, :], c1[:, 0:1, :]).then_inc(ln2.stored, 16)
            pool.wait_ge(ln2.stored, 16 * (BATCHES + 1))
            edge_pass(lin, lin_table, lambda s, j: gat[:, s, j, :], msg_ready, 2)

        @block.scalar
        def _(act):
            mine = act.alloc_register("act_steps")
            act.reg_mov(mine, 0)

            def step(ins):
                ins.then_inc(act_done, 1)
                act.reg_add(mine, mine, 1)
                act.wait_ge(act_done, mine)

            act.wait_ge(raw_loaded, 16 * 6)
            act.wait_ge(turned, 4)
            act.activation(raw_f[:, :, :], raw_s[:, :, :], ACT.Copy).then_inc(raw_fp, 1)

            def transposes_out(nd, c, n):
                act.wait_ge(nd.turned, c + 1)
                act.activation(cht[0:n, :, :], pa_f[0:n, 0:CB * P].rearrange("p (b q) -> p b q", q=P),
                               ACT.Copy).then_inc(nd.ht, 1)

            act.wait_ge(pool_consts, N_POOL)
            act.wait_ge(x_loaded, 32)

            def row_sums(func, to, bias):
                for junk, first, end in ((unused[0], 0, LATE), (unused[1], LATE, CHUNKS)):
                    with act.Fori(first, end) as c:
                        for j in range(CB):
                            b = c * CB + j
                            last = act.activation(junk[:, bass.ds(b - first * CB, 1), :], xr[:, bass.ds(b, 1), :], func,
                                                  bias=bias(b), accum_out=to[:, bass.ds(b, 1)])
                        last.then_inc(ln1.var, 1)
            row_sums(ACT.Copy, neg_mean, lambda b: 0.0)
            act.wait_ge(ln1.var, CHUNKS)
            step(act.activation(neg_mean[:, :], neg_mean[:, :], ACT.Copy, scale=-1.0 / F))
            row_sums(ACT.Square, std1, lambda b: neg_mean[:, bass.ds(b, 1)])
            act.wait_ge(ln1.var, 2 * CHUNKS)
            act.activation(std1[:, :], std1[:, :], ACT.Sqrt, bias=eps_col[:, :], scale=1.0 / F).then_inc(ln1.std, 1)

            with act.Fori(0, CHUNKS) as c:
                for j in range(CB):
                    b = c * CB + j
                    last = act.activation(hch[:, j:j + 1, :], xr[:, bass.ds(b, 1), :], ACT.Relu, bias=neg_mean[:, bass.ds(b, 1)])
                last.then_inc(ln1.h, 1)
                transposes_out(ln1, c, P)
                act.wait_ge(ln1.mm, c + 1)
                act.activation(tmsg[:, bass.ds(c * CB, CB), :],
                               pb[:, 0, 0:CB * HID].rearrange("p (b q) -> p b q", q=HID), ACT.Copy).then_inc(ln1.out, 1)
            act.wait_ge(deg_ready, 1)
            act.activation(deg_sb[:, :], deg_ps, ACT.Sqrt, bias=1.0).then_inc(deg_ready, 1)

            def split_parts(i):
                for h, blocks in enumerate(TABLE_HALVES):
                    act.wait_ge(tm_ready, 2 * i + h + 1)
                    act.activation(table_sb[:, blocks, part_of(0)], tmsg[:, blocks, :], ACT.Copy).then_inc(hi_ready, 1)
                for h, blocks in enumerate(TABLE_HALVES):
                    act.wait_ge(rest_ready, 2 * i + h + 1)
                    act.activation(table_sb[:, blocks, part_of(1)], agg_gcn[:, blocks, part_of(0)], ACT.Copy).then_inc(mid_ready, 1)
            split_parts(0)

            def next_idx(ps, g, s):
                act.activation(idx[:, s, :], idx_all[:, bass.ds(g * U, U)], ACT.Copy).then_inc(ps.idx_ready, 1)

            def first_idx(ps):
                for s in range(RING):
                    next_idx(ps, s, s)

            def after_gather(ps, it, s):
                act.wait_ge(ps.gathered[s], (it + 1) * (16 * U))
                next_idx(ps, (it + 1) * RING + s, s)

            act.sem_inc(win_out, 2)
            act.sem_inc(adj_stored[0], 1)
            act.sem_inc(adj_stored[1], 1)
            act.sem_inc(sums_out[0], 2)
            act.sem_inc(sums_out[1], 2)

            def sums_copy(i, b, bank):
                act.wait_ge(sums_ready[i], b + 1)
                act.activation(agg_gcn[:, bass.ds(b, 1), :].rearrange("p a c -> p (a c)"), bank[:, 0:TW],
                               ACT.Copy).then_inc(sums_out[i], 1)

            def build_block(b, i, k, stored, first=False):
                if not first:
                    act.wait_ge(adj_stored[i], stored + 1)
                for w in range(WB):
                    n = b * WB + w
                    act.wait_ge(win_ready, n + 1)
                    act.activation(adj[i][:, w * WC:(w + 1) * WC].rearrange("p (h c) -> p h c", h=2),
                                   win_ps[w % 2][:, :, 0:WC // 2], ACT.Copy,
                                   accum_out=counts[:, bass.ds(n, 1)]).then_inc(win_out, 1)
                    if w == 1 and not first:
                        act.wait_ge(key_used[1 - i], k + 1)
                        act.sem_inc(passed, 1)
                        act.activation(keys[1 - i], keys[1 - i], ACT.Copy, bias=float(-2 * P * NB)).then_inc(key_ready[1 - i], 1)
                if not first:
                    sums_copy(0, b - 1, sums[1 - i])
            act.wait_ge(shared_free, 1)
            act.wait_ge(ln1.mm, CHUNKS)
            act.activation(keys[1], keys[0], ACT.Copy, bias=float(-P * NB)).then_inc(key_ready[1], 1)
            build_block(0, 0, 0, 0, first=True)
            with act.Fori(0, NB // 2) as it:
                build_block(it * 2 + 1, 1, it, it * 16)
                build_block(it * 2 + 2, 0, it, it * 16 + 16)
            sums_copy(0, NB - 1, sums[0])

            act.wait_ge(over_ready, 1)
            over = act.alloc_register("over_act")
            act.load(over, over_i[0:1, 0:1])

            def gather_idx(i):
                first_idx(gcn[i])
                with act.Fori(0, ITERS - 1) as it:
                    for s in range(RING):
                        after_gather(gcn[i], it, s)
                for s in range(RING):
                    act.wait_ge(gcn[i].gathered[s], ITERS * 16 * U)
            def batch_turned(nd, i, k, n, rows):
                act.wait_ge(nd.turned, k + 1)
                act.activation(bt[i][0:rows, 0:n, :], pa[0:rows, i, 0:n * P].rearrange("p (b q) -> p b q", q=P),
                               ACT.Copy).then_inc(nd.ht, 1)

            def batch_std(k, n):
                act.wait_ge(ln2.var, k + 1)
                act.activation(st[:, 2, 0:n], st[:, 1, 0:n], ACT.Sqrt, bias=eps_col[:, :], scale=1.0 / F).then_inc(ln2.std, 1)

            def batch_out(k, n):
                act.wait_ge(ln2.mm, k + 1)
                act.wait_ge(rows_free, k + 1)
                act.activation(c1[:, 0:n, :], pb[:, 1, 0:n * F].rearrange("p (b q) -> p b q", q=F), ACT.Copy).then_inc(ln2.out, 1)

            def batch_steps(k, n):
                batch_turned(lin2, 0, k, n, HID)
                batch_std(k, n)
                batch_turned(ln2, 1, k, n, P)
                batch_out(k, n)

            with act.If_ne(over, 0):
                gather_idx(0)
                split_parts(1)
                gather_idx(1)
                with act.Fori(0, BATCHES) as k:
                    batch_steps(k, RB)
            with act.Else():
                split_parts(1)
                act.wait_ge(split_ready[1], 2)

                def copies(i, last_batch=True, one_before=True):
                    sums_copy(1, i * RB, sums[0])
                    if one_before:
                        batch_out(i - 2, RB)
                    if last_batch:
                        batch_turned(lin2, 0, i - 1, RB, HID)
                    sums_copy(1, i * RB + 1, sums[1])
                    sums_copy(1, i * RB + 2, sums[0])
                    if last_batch:
                        batch_std(i - 1, RB)
                    sums_copy(1, i * RB + 3, sums[1])
                    if last_batch:
                        batch_turned(ln2, 1, i - 1, RB, P)
                copies(0, last_batch=False, one_before=False)
                copies(1, one_before=False)
                with act.Fori(2, BATCHES) as i:
                    copies(i)
                sums_copy(1, NB - 1, sums[0])
                batch_out(BATCHES - 2, RB)
                batch_steps(BATCHES - 1, RB)
            batch_steps(BATCHES, 1)

            def edge_act(g):
                act.wait_ge(ea_turned, g + 1)
                act.wait_ge(hid_mm, g * 2)
                act.activation(ea_t[:, :], pd[:, :], ACT.Copy).then_inc(ea_out, 1)
                for h in range(2):
                    act.wait_ge(hid_mm, g * 2 + (h + 1))
                    if not isinstance(g, int) or g > 0:
                        act.wait_ge(w_mm, g * 2 + (h - 1))
                    act.activation(act_t[:, h, :], pa[:, h, :], ACT.Silu, bias=be1_col[:, :]).then_inc(hid_act, 1)

            first_idx(lin)
            edge_act(0)
            with act.Fori(0, ITERS - 1) as it:
                for s in range(RING):
                    edge_act(it * RING + (s + 1))
                    after_gather(lin, it, s)
            for s in range(RING - 1):
                edge_act((ITERS - 1) * RING + s + 1)

            def mlp_turned(k, n):
                act.wait_ge(up.turned, k + 1)
                if k > 1:
                    act.wait_ge(up.mm, k - 1)
                act.activation(bt[k % 2][:, 0:n, :], pa[:, k % 2, 0:n * P].rearrange("p (b q) -> p b q", q=P),
                               ACT.Copy).then_inc(up.ht, 1)

            def mlp_silu(k, n):
                act.wait_ge(up.mm, k + 1)
                if k > 1:
                    act.wait_ge(down.mm, k - 1)
                act.activation(hid[k % 2][:, 0:n, :], pb[:, k % 2, 0:n * P].rearrange("p (b q) -> p b q", q=P), ACT.Silu,
                               bias=bn1_col[:, :]).then_inc(up.out, 1)

            mlp_turned(0, RB)
            for k in range(1, BATCHES + 1):
                mlp_turned(k, RB if k < BATCHES else 1)
                mlp_silu(k - 1, RB)
            mlp_silu(BATCHES, 1)

        @block.vector
        def _(dve):
            mine = dve.alloc_register("dve_steps")
            dve.reg_mov(mine, 0)

            def step(ins):
                ins.then_inc(dve_done, 1)
                dve.reg_add(mine, mine, 1)
                dve.wait_ge(dve_done, mine)

            def bc(ap, n):
                return ap.rearrange("p (b a) -> p b a", a=1).to_broadcast([P, ap.shape[1], n])

            def lanes(t, g, n):
                return t[:, bass.ds(g * U, U)].rearrange("p (a u) -> p a u", a=1).to_broadcast([P, n, U])

            dve.wait_ge(pool_consts, N_POOL - 1)
            step(dve.tensor_copy(iota_f[:, :], iota_i[:, :]))
            step(dve.tensor_copy(iota_u[:, :, :], bc(iota_i[:, :], U)))
            step(dve.tensor_copy(iota_t[:, :, :], bc(iota_i[:, :], T)))
            step(dve.tensor_copy(neg_base[:, :], base_i[:, :]))
            step(dve.tensor_copy(col_h[:, :], col_i[:, :]))
            step(dve.tensor_copy(win_f[:, :], win_i[:, :]))

            dve.wait_ge(raw_loaded, 16 * 6)
            dve.tensor_copy(raw_f[:, :, :], raw_d[:, :, :]).then_inc(raw_fp, 1)
            by_unit = raw_d.rearrange("p k (q e) -> p (k q) e", q=Q)
            for m, op in enumerate((ALU.min, ALU.max)):
                step(dve.tensor_reduce(um_i[:, m, :], by_unit, AX.X, op))
                step(dve.tensor_reduce(mm_i[:, m * HALVES:(m + 1) * HALVES],
                                       um_i[:, m, :].rearrange("p (k q) -> p k q", q=Q), AX.X, op))
            step(dve.tensor_scalar(um_i[:, :, :], um_i[:, :, :], 4, None, ALU.arith_shift_right))
            step(dve.tensor_copy(um_f[:, :, :], um_i[:, :, :]))
            dve.tensor_copy(um_w[:, :, :], bc(um_f[:, :, :].rearrange("p m c -> p (m c)"), WP)).then_inc(um_ready, 1)
            step(dve.tensor_scalar(mm_i[:, :], mm_i[:, :], 7, None, ALU.arith_shift_right))
            step(dve.tensor_copy(mm_f[:, :], mm_i[:, :]))
            dve.tensor_scalar(mm_f[:, HALVES:2 * HALVES], mm_f[:, HALVES:2 * HALVES], 1.0, None, ALU.add).then_inc(mm_ready, 1)
            dve.wait_ge(row_ready, 1)
            dve.tensor_copy(bounds[:, :].rearrange("a (g m) -> a m g", m=2), row_ps.rearrange("a (m g) -> a m g", m=2)).then_inc(bounds_ready, 1)

            def turned_copy(n, m, to):
                k, r = m // 2, m % 2
                gs = P if k == 0 else G1
                view = to[:, k * GE:k * GE + gs * U].rearrange("p (g j) -> p j g", j=U)[:, 4 * r:4 * r + 4, :]
                dve.wait_ge(turned, n + 1)
                dve.tensor_copy(view, banks[m].rearrange("p (j g) -> p j g", g=P)[:, :, 0:gs]).then_inc(turned_out, 1)
            for m in range(4):
                turned_copy(m, m, dst_f[:, :])
            for m in range(4):
                turned_copy(4 + m, m, idx_all[:, :])
            dve.wait_ge(turned_out, 8)
            step(dve.tensor_copy(dst_i, dst_f[:, :]))
            step(dve.tensor_scalar(tmp_i, dst_i, P - 1, None, ALU.bitwise_and))
            step(dve.tensor_copy(dlo, tmp_i))
            step(dve.tensor_scalar(tmp_i, dst_i, 7, None, ALU.arith_shift_right))
            step(dve.tensor_copy(dhi, tmp_i))
            step(dve.tensor_scalar(tmp_i, idx_all[:, :], P - 1, None, ALU.bitwise_and))
            step(dve.tensor_copy(src_lo, tmp_i))
            step(dve.tensor_scalar(tmp_i, idx_all[:, :], 7, None, ALU.arith_shift_right))
            dve.scalar_tensor_tensor(keys[0], dst_f[:, :], float(NB), tmp_i, ALU.mult, ALU.add).then_inc(shared_free, 1)
            dve.sem_inc(key_ready[0], 1)
            dve.wait_ge(shared_free, 1)

            dve.wait_ge(um_rows, 1)
            some = c0[0:WP, :, :].rearrange("p b f -> p (b f)")[:, 0:UNITS]
            which = c1[0:WP, :, :].rearrange("p b f -> p (b f)")[:, 0:UNITS]
            for i in range(4):
                step(dve.tensor_scalar(some, pa_f[0:WP, 0:UNITS], win_f[0:WP, i:i + 1], None, ALU.is_le))
                step(dve.scalar_tensor_tensor(some, pb_f[0:WP, 0:UNITS], win_f[0:WP, i:i + 1], some, ALU.is_ge, ALU.mult))
                step(dve.scalar_tensor_tensor(which, unit_i[0:WP, :], float(-FAR), some, ALU.add, ALU.mult))
                step(dve.tensor_reduce(win_lo[0:WP, i:i + 1], which, AX.X, ALU.min))
                step(dve.scalar_tensor_tensor(which, unit_i[0:WP, :], 1.0, some, ALU.add, ALU.mult))
                step(dve.tensor_reduce(win_hi[0:WP, i:i + 1], which, AX.X, ALU.max))
            step(dve.tensor_scalar(win_lo[0:WP, :], win_lo[0:WP, :], float(FAR + 2), float(UNITS), ALU.add, ALU.min))
            dve.tensor_tensor(win_hi[0:WP, :], win_hi[0:WP, :], win_lo[0:WP, :], ALU.max).then_inc(win_cols, 1)
            step(dve.memset(windows[:, NB:NB + 1, :, :], 0))
            dve.wait_ge(win_rows, 1)
            for m in range(2):
                dve.tensor_copy(windows[:, 0:NB, m, :], pa[0:1, m, 0:NW].rearrange("a (b w) -> a b w", w=WB)).then_inc(windows_ready, 1)

            dve.wait_ge(w_loaded, 16 * (N_W - 3))
            dve.wait_ge(pool_consts, N_POOL)
            step(dve.tensor_copy(be2_hi[:, :], be2_rows[:, :]))
            step(dve.tensor_tensor(be2_res[:, :], be2_rows[:, :], be2_hi[:, :], ALU.subtract))
            step(dve.tensor_copy(be2_mid[:, :], be2_res[:, :]))
            step(dve.tensor_tensor(be2_lo[:, :], be2_res[:, :], be2_mid[:, :], ALU.subtract))
            step(dve.tensor_scalar(be2_res[:, :], be2_hi[:, :], ident[0:PARTS, 0:1], None, ALU.mult))
            step(dve.scalar_tensor_tensor(be2_res[:, :], be2_mid[:, :], ident[0:PARTS, 1:2], be2_res[:, :], ALU.mult, ALU.add))
            step(dve.scalar_tensor_tensor(be2_res[:, :], be2_lo[:, :], ident[0:PARTS, 2:3], be2_res[:, :], ALU.mult, ALU.add))
            for i in range(4):
                dve.tensor_copy(be2_parts[:, i, :], be2_res[:, :]).then_inc(consts, 1)

            with dve.Fori(0, ITERS * RING // 2) as it:
                for s in range(2):
                    g = it * 2 + s
                    dve.wait_ge(hist_used, it * 2 + (s + 1))
                    dve.tensor_tensor(hist_lo[:, s, :, :], iota_u[:, :, :], lanes(dlo, g, P), ALU.is_equal)\
                       .then_inc(hist_hot, 1)
                    dve.tensor_tensor(hist_hi[:, s, :, :], iota_u[:, 0:NB, :], lanes(dhi, g, NB), ALU.is_equal)\
                       .then_inc(hist_hot, 1)
            dve.wait_ge(deg_ready, 2)
            step(dve.reciprocal(dinv[:, :], deg_sb[:, :]))
            dve.wait_ge(ln1.std, 1)
            step(dve.reciprocal(std1[:, :], std1[:, :]))
            step(dve.tensor_tensor(std1[:, :], std1[:, :], dinv[:, :], ALU.mult))
            dve.sem_inc(passed, 1)

            def split_rest(i):
                for h, blocks in enumerate(TABLE_HALVES):
                    dve.wait_ge(hi_ready, 2 * i + h + 1)
                    dve.tensor_tensor(agg_gcn[:, blocks, part_of(0)], tmsg[:, blocks, :], table_sb[:, blocks, part_of(0)],
                                      ALU.subtract).then_inc(rest_ready, 1)
                for h, blocks in enumerate(TABLE_HALVES):
                    dve.wait_ge(mid_ready, 2 * i + h + 1)
                    dve.tensor_tensor(table_sb[:, blocks, part_of(2)], agg_gcn[:, blocks, part_of(0)],
                                      table_sb[:, blocks, part_of(1)], ALU.subtract).then_inc(split_ready[i], 1)
                dve.wait_ge(split_ready[i], 2)

            dve.wait_ge(ln1.out, CHUNKS)
            for blocks in TABLE_HALVES:
                tm = tmsg[:, blocks, :]
                dve.tensor_tensor(tm, tm, bc(std1[:, blocks], HID), ALU.mult).then_inc(tm_ready, 1)
            split_rest(0)

            pairs = dve.alloc_register("pairs_dve")
            span = [dve.alloc_register(f"span_dve{i}") for i in range(2)]
            dve.wait_ge(bounds_ready, 1)

            def gcn_pass(ps):
                dve.reg_mov(pairs, 0)
                dve.sem_inc(ps.added, 1)
                with dve.Fori(0, G) as g:
                    first, end = group_blocks(dve, span, g)
                    with dve.Fori(first, end) as b:
                        step(dve.tensor_scalar(dl_b[:, :], dst_f[:, bass.ds(g * U, U)], neg_base[:, bass.ds(b, 1)], None, ALU.add))
                        dve.tensor_tensor(hot_b, iota_u[:, :, :],
                                          dl_b[:, :].rearrange("p (a u) -> p a u", a=1).to_broadcast([P, P, U]),
                                          ALU.is_equal).then_inc(ps.hot, 1)
                        dve.reg_add(pairs, pairs, 1)
                        dve.wait_ge(ps.summed, pairs)
                        a = agg_gcn[:, bass.ds(b, 1), :].rearrange("p a c -> p (a c)")
                        dve.tensor_tensor(a, a, pc[:, 0:TW], ALU.add).then_inc(ps.added, 1)
                    dve.sem_inc(ps.rows_used, 1)
                dve.reg_add(pairs, pairs, 1)
                dve.wait_ge(ps.added, pairs)
                dve.sem_inc(passed, 1)

            units = dve.alloc_register("units_dve")
            dve.reg_mov(units, 1)
            for t in range(T):
                dve.sem_inc(tile_hot[t], 1)
            ranges = [[dve.alloc_register(f"range_dve{i}_{n}") for n in range(2 * WB)] for i in range(2)]
            dve.wait_ge(windows_ready, 2)

            def columns(to, i, tile, w):
                return dve.tensor_scalar(to, col_h[:, :], keys[i][:, bass.ds(tile, 1)], float(-WC * w), ALU.subtract, ALU.is_equal)

            def sources(to, iota, tile, n):
                return dve.tensor_tensor(to[:, :, :], iota[:, :, :],
                                         src_lo[:, bass.ds(tile, n)].rearrange("p (a t) -> p a t", a=1).to_broadcast([P, P, n]),
                                         ALU.is_equal)

            def build_block(b, i, k, first=False):
                spans = ranges[i]
                dve.wait_ge(key_ready[i], k + 1)
                dve.sem_inc(passed, 1)
                for w in range(WB):
                    third = dve.snap(spans[w], min_val=2, max_val=UNITS)
                    tile = third * T - 2 * T
                    sources(head_lo[w % 2], iota_u[:, :, 0:2 * T], tile, 2 * T)
                    for j in range(2):
                        dve.wait_ge(head_used[j], b * WB + (w + 1))
                        for t in range(T):
                            columns(head_col[j][:, t, :], i, tile + j * T + t, w).then_inc(head_hot[j], 1)
                    if w == 0 and not first:
                        dve.wait_ge(head_hot[1], b * (WB * T))
                        dve.sem_inc(passed, 1)
                        dve.wait_ge(tile_hot[T - 1], units)
                        dve.sem_inc(key_used[1 - i], 1)
                    with dve.If_lt(spans[w], spans[WB + w]):
                        with dve.Fori(third, dve.snap(spans[WB + w], min_val=3, max_val=UNITS)) as u:
                            dve.reg_add(units, units, 1)
                            dve.wait_ge(tile_used[0], units)
                            columns(loop_col[:, 0, :], i, u * T, w)
                            dve.wait_ge(tile_used[1], units)
                            sources(loop_lo, iota_t, u * T, T).then_inc(tile_hot[0], 1)
                            columns(loop_col[:, 1, :], i, u * T + 1, w).then_inc(tile_hot[1], 1)
                    if w == WB // 2:
                        window_spans(dve, ranges[1 - i], b + 1)

            window_spans(dve, ranges[0], 0)
            build_block(0, 0, 0, first=True)
            with dve.Fori(0, NB // 2) as it:
                build_block(it * 2 + 1, 1, it)
                build_block(it * 2 + 2, 0, it + 1)

            dve.wait_ge(key_ready[1], NB // 2 + 1)
            dve.wait_ge(win_out, NW + 2)
            dve.tensor_reduce(most[:, :], counts[:, :], AX.X, ALU.max).then_inc(most_ready, 1)
            dve.wait_ge(most_row, 1)
            step(dve.tensor_reduce(over_f[:, :], pa[0:1, 0, 0:P], AX.X, ALU.max))
            dve.tensor_scalar(over_i[:, :], over_f[:, :], float(EXACT), None, ALU.is_ge).then_inc(over_ready, 1)
            dve.wait_ge(over_ready, 1)
            over = dve.alloc_register("over_dve")
            dve.load(over, over_i[0:1, 0:1])

            dve.wait_ge(sums_out[0], NB + 2)
            with dve.If_ne(over, 0):
                step(dve.memset(agg[:, :], 0.0))
                dve.sem_inc(passed, 1)
                gcn_pass(gcn[0])
                dve.wait_ge(table_stored[0], 16)

            def gcn_sum(first, n, to):
                blocks = bass.ds(first, n)
                a = agg_gcn[:, blocks, :]
                tm = tmsg[:, blocks, :]
                s0 = c0[:, 0:n, 0:HID]
                step(dve.tensor_tensor(s0, a[:, :, 0:HID], a[:, :, HID:2 * HID], ALU.add))
                step(dve.tensor_tensor(s0, s0, a[:, :, 2 * HID:3 * HID], ALU.add))
                step(dve.tensor_tensor(s0, s0, tm, ALU.add))
                return dve.tensor_tensor(to, s0, bc(dinv[:, blocks], HID), ALU.mult)

            def all_rows(ap, n):
                return ap.rearrange("p (a c) -> p a c", a=1).to_broadcast([P, n, ap.shape[1]])

            for blocks in TABLE_HALVES:
                n = blocks.stop - blocks.start
                tm, a = tmsg[:, blocks, :], agg_gcn[:, blocks, :]
                total = a[:, :, part_of(0)]
                step(dve.tensor_tensor(total, total, a[:, :, part_of(1)], ALU.add))
                step(dve.tensor_tensor(total, total, a[:, :, part_of(2)], ALU.add))
                step(dve.tensor_tensor(total, total, tm, ALU.add))
                step(dve.tensor_tensor(total, total, bc(dinv[:, blocks], HID), ALU.mult))
                step(dve.tensor_tensor(total, total, all_rows(b1_all[:, :], n), ALU.add))
                dve.scalar_tensor_tensor(tm, total, 0.0, bc(dinv[:, blocks], HID), ALU.max, ALU.mult).then_inc(tm_ready, 1)
            dve.wait_ge(tm_ready, 4)
            split_rest(1)
            with dve.If_ne(over, 0):
                step(dve.memset(agg[:, :], 0.0))
                dve.sem_inc(passed, 1)
                gcn_pass(gcn[1])
                dve.sem_inc(sums_out[1], NB)
            dve.sem_inc(ea_clean, 1)

            def batch(k, n):
                rows = xr[:, bass.ds(k * RB, n), :]
                dve.wait_ge(sums_out[1], k * RB + (n + 2))
                dve.sem_inc(passed, 1)
                gcn_sum(k * RB, n, hch_in[:, 0:n, :]).then_inc(lin2.h, 1)
                step(dve.tensor_tensor(rows, rows, all_rows(b2_all[:, :], n), ALU.add))
                dve.wait_ge(lin2.mm, k + 1)
                step(dve.tensor_tensor(rows, rows, pb[:, 0, 0:n * F].rearrange("p (b q) -> p b q", q=F), ALU.add))
                dve.sem_inc(lin2.out, 1)
                x0, h = c0[:, 0:n, :], hch[:, 0:n, :]
                step(dve.tensor_reduce(st[:, 0, 0:n], rows, AX.X, ALU.add))
                step(dve.tensor_scalar(st[:, 0, 0:n], st[:, 0, 0:n], -1.0 / F, None, ALU.mult))
                step(dve.tensor_tensor(x0, rows, bc(st[:, 0, 0:n], F), ALU.add))
                step(dve.tensor_tensor(sq[:, 0:n, :], x0, x0, ALU.mult))
                dve.tensor_reduce(st[:, 1, 0:n], sq[:, 0:n, :], AX.X, ALU.add).then_inc(ln2.var, 1)
                dve.wait_ge(ln2.std, k + 1)
                step(dve.reciprocal(st[:, 3, 0:n], st[:, 2, 0:n]))
                dve.scalar_tensor_tensor(h, x0, 0.0, bc(st[:, 3, 0:n], F), ALU.max, ALU.mult).then_inc(ln2.h, 1)
                dve.wait_ge(ln2.h, k + 1)
                step(dve.tensor_tensor(rows, rows, h, ALU.add))
                step(dve.tensor_tensor(rows, rows, all_rows(bn2_all[:, :], n), ALU.add))

            with dve.Fori(0, BATCHES) as k:
                batch(k, RB)
            batch(BATCHES, 1)
            step(dve.memset(agg[:, 0:NB * F], 0.0))
            dve.sem_inc(passed, 1)

            dve.reg_mov(pairs, 0)
            dve.sem_inc(lin.added, 1)

            def messages(g, turns, s):
                rows = gat[:, s, :, :].rearrange("p (i h) f -> p h i f", h=2)
                dve.wait_ge(lin.gathered[s], turns * (16 * U))
                dve.sem_inc(passed, 1)
                for h in range(2):
                    dve.wait_ge(w_mm, g * 2 + (h + 1))
                    dve.tensor_tensor(msg[:, h, :, :], pb[:, h, :].rearrange("p (i f) -> p i f", f=F),
                                      rows[:, h, :, :], ALU.mult).then_inc(msg_ready, 1)

            def group_sums(g):
                first, end = group_blocks(dve, span, g)
                with dve.Fori(first, end) as b:
                    step(dve.tensor_scalar(dl_f[:, :], dst_f[:, bass.ds(g * U, U)], neg_base[:, bass.ds(b, 1)], None, ALU.add))
                    dve.tensor_tensor(hot_f[:, :, :], iota_f[:, :].rearrange("p (a d) -> p a d", a=1).to_broadcast([P, U, P]),
                                      bc(dl_f[:, :], P), ALU.is_equal).then_inc(lin.hot, 1)
                    dve.reg_add(pairs, pairs, 1)
                    dve.wait_ge(lin.summed, pairs)
                    a = agg_lin[:, bass.ds(b, 1), :].rearrange("p a c -> p (a c)")
                    dve.tensor_tensor(a, a, pc[:, 0:F], ALU.add).then_inc(lin.added, 1)

            messages(0, 1, 0)
            with dve.Fori(0, ITERS - 1) as it:
                for s in range(1, RING + 1):
                    g = it * RING + s
                    group_sums(g - 1)
                    messages(g, it + (s // RING + 1), s % RING)
            for s in range(1, RING):
                g = (ITERS - 1) * RING + s
                group_sums(g - 1)
                messages(g, ITERS, s)
            group_sums(G - 1)
            for k in range(BATCHES + 1):
                n = RB if k < BATCHES else 1
                rows = xr[:, k * RB:k * RB + n, :]
                dve.wait_ge(down.mm, k + 1)
                dve.tensor_tensor(rows, rows, mlp_out[k % 2][:, 0:n * F].rearrange("p (b q) -> p b q", q=F),
                                  ALU.add).then_inc(down.out, 1)

        @block.tensor
        def _(pe):
            pe.wait_ge(pool_consts, N_POOL)
            for a in range(2):
                pe.wait_ge(raw_fp, a + 1)
                for k in range(HALVES):
                    for r in range(2):
                        n = 2 * k + r
                        if a == 1:
                            pe.wait_ge(turned_out, n + 1)
                        cols = raw_f[:, k, :]
                        for j in range(4):
                            q, t = divmod(4 * r + j, T)
                            edges = cols[:, q * UE:(q + 1) * UE].rearrange("p (e t) -> p t e", t=T)[:, t, :]
                            last = pe.transpose(banks[n][:, j * P:(j + 1) * P], edges, ident[:, :])
                        last.then_inc(turned, 1)
                if a == 0:
                    pe.wait_ge(mm_ready, 1)
                    for i in range(2 * HALVES):
                        last = pe.matmul(pc[0:1, i * P:(i + 1) * P], mm_f[:, i:i + 1], ident[:, :], start=True, stop=True)
                    last.then_inc(row_ready, 1)

            pe.wait_ge(um_ready, 1)
            pe.wait_ge(turned_out, 8)
            for m, to in enumerate((pa_f, pb_f)):
                at = 0
                for k in range(HALVES):
                    gs = P if k == 0 else G1
                    for q in range(Q):
                        last = pe.matmul(to[0:WP, at:at + gs], um_w[:, (m * HALVES + k) * Q + q, :], ident[:, 0:gs],
                                         start=True, stop=True)
                        at += gs
            last.then_inc(um_rows, 1)
            pe.wait_ge(win_cols, 1)
            for m, cols in enumerate((win_lo, win_hi)):
                for i in range(4):
                    last = pe.matmul(pa[0:1, m, i * WP:(i + 1) * WP], cols[0:WP, i:i + 1], ident[0:WP, 0:WP],
                                     start=True, stop=True)
            last.then_inc(win_rows, 1)

            def turn(nd, c, rows, n):
                pe.wait_ge(nd.h, c + 1)
                pe.sem_inc(passed, 1)
                for j in range(CB):
                    last = pe.transpose(pa_f[0:n, j * P:(j + 1) * P], rows(j), ident[:, :])
                last.then_inc(nd.turned, 1)

            pe.wait_ge(w_loaded, 16 * (N_W - 3))
            pe.wait_ge(windows_ready, 2)

            pe.sem_inc(hist_used, 1)
            pe.matmul(deg_ps, zeros_b[:, :], zeros_b[:, 0:NB], start=True, stop=False).then_inc(hist_used, 1)
            HIST = G // (2 * 2 * CHUNKS)
            assert HIST * 2 * 2 * CHUNKS == G

            def histogram(first):
                with pe.Fori(0, HIST) as i:
                    for s in range(2):
                        pe.wait_ge(hist_hot, (first * HIST + i) * 4 + (2 * s + 2))
                        for u in range(U):
                            last = pe.matmul(deg_ps, hist_lo[:, s, :, u], hist_hi[:, s, :, u], start=False, stop=False)
                        last.then_inc(hist_used, 1)

            with pe.Fori(0, CHUNKS) as c:
                turn(ln1, c, lambda j: hch[:, j, :], P)
                histogram(c * 2)
                pe.wait_ge(ln1.ht, c + 1)
                for j in range(CB):
                    last = pe.matmul(pb[:, 0, j * HID:(j + 1) * HID], cht[:, j, :], w1_sb[:, :], start=True, stop=True)
                last.then_inc(ln1.mm, 1)
                histogram(c * 2 + 1)
            pe.matmul(deg_ps, zeros_b[:, :], zeros_b[:, 0:NB], start=False, stop=True).then_inc(deg_ready, 1)

            units = pe.alloc_register("units_pe")
            pe.reg_mov(units, 1)
            ranges = [pe.alloc_register(f"range_pe{i}") for i in range(2 * WB)]
            for t in range(T):
                pe.sem_inc(tile_used[t], 2)
                pe.sem_inc(head_used[t], 1)

            def edge_sum(ps, first):
                for h in range(2):
                    last = pe.matmul(ps[:, h, 511:512], zeros_b[:, :], zeros_b[:, 0:1], start=first, stop=not first)
                return last

            def convolve(i, b, block, bank, blocks=range(NB)):
                if blocks[0] == 0:
                    pe.wait_ge(sums_out[i], b + 1)
                    pe.sem_inc(passed, 1)
                by_source = block.rearrange("p (d h) -> p h d", h=NB)
                for h in blocks:
                    last = pe.matmul(bank[:, 0:TW], by_source[:, h, :], table_sb[:, h, :], start=(h == 0), stop=(h == NB - 1))
                if blocks[-1] == NB - 1:
                    last.then_inc(sums_ready[i], 1)

            def tile_counts(ps, lo, col):
                for h in range(2):
                    last = pe.matmul(ps[:, h, 0:WC // 2], lo, col[:, h * WC // 2:(h + 1) * WC // 2], start=False, stop=False)
                return last

            def build_block(b, i, first=False):
                window_spans(pe, ranges, b)
                for w in range(WB):
                    ps = win_ps[w % 2]
                    pe.wait_ge(win_out, b * WB + w + 1)
                    pe.sem_inc(passed, 1)
                    edge_sum(ps, True)
                    for j in range(2):
                        for t in range(T):
                            pe.wait_ge(head_hot[j], (b * WB + w) * T + (t + 1))
                            last = tile_counts(ps, head_lo[w % 2][:, :, j * T + t], head_col[j][:, t, :])
                        last.then_inc(head_used[j], 1)
                    with pe.If_lt(ranges[w], ranges[WB + w]):
                        with pe.Fori(ranges[w], ranges[WB + w]):
                            pe.reg_add(units, units, 1)
                            for t in range(T):
                                pe.wait_ge(tile_hot[t], units)
                                tile_counts(ps, loop_lo[:, :, t], loop_col[:, t, :]).then_inc(tile_used[t], 1)
                    edge_sum(ps, False).then_inc(win_ready, 1)
                    if w > 0 and not first:
                        convolve(0, b - 1, adj[1 - i], sums[1 - i], range((w - 1) * NB // (WB - 1), w * NB // (WB - 1)))

            pe.wait_ge(ln1.out, CHUNKS)
            pe.wait_ge(deg_ready, 2)
            build_block(0, 0, first=True)
            pe.wait_ge(split_ready[0], 2)
            with pe.Fori(0, NB // 2) as it:
                build_block(it * 2 + 1, 1)
                build_block(it * 2 + 2, 0)
            pe.wait_ge(win_out, NW + 2)
            convolve(0, NB - 1, adj[0], sums[0])
            pe.wait_ge(most_ready, 1)
            pe.transpose(pa[0:1, 0, 0:P], most[:, :], ident[:, :]).then_inc(most_row, 1)

            pairs = pe.alloc_register("pairs_pe")
            span = [pe.alloc_register(f"span_pe{i}") for i in range(2)]
            pe.wait_ge(bounds_ready, 1)
            pe.wait_ge(over_ready, 1)
            over = pe.alloc_register("over_pe")
            pe.load(over, over_i[0:1, 0:1])

            def gcn_pass(ps):
                pe.reg_mov(pairs, 0)
                with pe.Fori(0, ITERS) as it:
                    for s in range(RING):
                        g = it * RING + s
                        first, end = group_blocks(pe, span, g)
                        pe.wait_ge(ps.gathered[s], (it + 1) * (16 * U))
                        pe.sem_inc(passed, 1)
                        with pe.Fori(first, end) as b:
                            pe.reg_add(pairs, pairs, 1)
                            pe.wait_ge(ps.added, pairs)
                            pe.sem_inc(passed, 1)
                            pe.wait_ge(ps.hot, pairs)
                            for u in range(U):
                                last = pe.matmul(pc[:, 0:TW], hot_b[:, :, u], gat_b[:, s, u * TW:(u + 1) * TW],
                                                 start=(u == 0), stop=(u == U - 1))
                            last.then_inc(ps.summed, 1)
            def batch_turn(nd, i, k, n, rows, to):
                pe.wait_ge(nd.h, k + 1)
                pe.sem_inc(passed, 1)
                for j in range(n):
                    last = pe.transpose(pa[0:to, i, j * P:(j + 1) * P], rows[:, j, :], ident[:, :])
                last.then_inc(nd.turned, 1)

            def batch_product(nd, i, k, n, rows, weights):
                pe.wait_ge(nd.ht, k + 1)
                for j in range(n):
                    last = pe.matmul(pb[:, i, j * F:(j + 1) * F], bt[i][0:rows, j, :], weights[:, :], start=True, stop=True)
                last.then_inc(nd.mm, 1)

            def sums_turn(k, n):
                batch_turn(lin2, 0, k, n, hch_in, HID)

            def sums_product(k, n):
                batch_product(lin2, 0, k, n, HID, w2_sb)

            def norm_turn(k, n):
                batch_turn(ln2, 1, k, n, hch, P)

            def norm_product(k, n):
                batch_product(ln2, 1, k, n, P, wlin_sb)

            def batch_steps(k, n):
                for stage in (sums_turn, sums_product, norm_turn, norm_product):
                    stage(k, n)

            with pe.If_ne(over, 0):
                gcn_pass(gcn[0])
                gcn_pass(gcn[1])
                with pe.Fori(0, BATCHES) as k:
                    batch_steps(k, RB)
            with pe.Else():
                pe.wait_ge(split_ready[1], 2)

                def convolve_batch(i, last_batch=True, one_before=True):
                    for j in range(RB):
                        pe.wait_ge(adj_loaded[j], i * 16 + 16)
                        convolve(1, i * RB + j, adj[j], sums[j % 2])
                        if j == 0 and one_before:
                            norm_product(i - 2, RB)
                        if j == 0 and last_batch:
                            sums_turn(i - 1, RB)
                        if j == 1 and last_batch:
                            sums_product(i - 1, RB)
                        if j == 3 and last_batch:
                            norm_turn(i - 1, RB)
                convolve_batch(0, last_batch=False, one_before=False)
                convolve_batch(1, one_before=False)
                with pe.Fori(2, BATCHES) as i:
                    convolve_batch(i)
                pe.wait_ge(adj_loaded[0], (BATCHES + 1) * 16)
                convolve(1, NB - 1, adj[0], sums[0])
                norm_product(BATCHES - 2, RB)
                batch_steps(BATCHES - 1, RB)
            batch_steps(BATCHES, 1)

            def turn_ea(g, turns, s):
                pe.wait_ge(ea_loaded[s], turns * 16)
                pe.wait_ge(ea_out, g)
                for i in range(4):
                    last = pe.transpose(pd[:, i * P:(i + 1) * P], ea[:, s, i * P:(i + 1) * P], ident[:, :])
                last.then_inc(ea_turned, 1)

            def layer1(g):
                pe.wait_ge(ea_out, g + 1)
                for h in range(2):
                    half = slice(h * RBF, (h + 1) * RBF)
                    pe.matmul(pa[:, h, :], we1_sb[half, :], ea_t[half, :], start=True, stop=True).then_inc(hid_mm, 1)

            def layer2(g):
                for h in range(2):
                    if not isinstance(g, int) or g > 0:
                        pe.wait_ge(msg_ready, g * 2 + (h - 1))
                        pe.sem_inc(passed, 1)
                    pe.matmul(pb[:, h, :], ones3[:, :], be2_parts[:, :, :].rearrange("p i f -> p (i f)"),
                              start=True, stop=False)
                    pe.wait_ge(hid_act, g * 2 + (h + 1))
                    for i in range(4):
                        last = pe.matmul(pb[:, h, i * F:(i + 1) * F], act_t[:, h, i * P:(i + 1) * P], we2_sb[:, :],
                                         start=False, stop=(i == 3))
                    last.then_inc(w_mm, 1)

            def group_sums(g):
                first, end = group_blocks(pe, span, g)
                pe.wait_ge(msg_ready, g * 2 + 2)
                pe.sem_inc(passed, 1)
                with pe.Fori(first, end) as b:
                    pe.reg_add(pairs, pairs, 1)
                    pe.wait_ge(lin.added, pairs)
                    pe.sem_inc(passed, 1)
                    pe.wait_ge(lin.hot, pairs)
                    for h in range(2):
                        for i in range(4):
                            last = pe.matmul(pc[:, 0:F], hot_f[:, 2 * i + h, :], msg[:, h, i, :],
                                             start=(h == 0 and i == 0), stop=(h == 1 and i == 3))
                    last.then_inc(lin.summed, 1)

            pe.wait_ge(consts, 4)
            pe.reg_mov(pairs, 0)
            turn_ea(0, 1, 0)
            layer1(0)
            turn_ea(1, 1, 1)
            layer2(0)
            layer1(1)
            with pe.Fori(0, ITERS - 1) as it:
                for s in range(1, RING + 1):
                    g = it * RING + s
                    turn_ea(g + 1, it + ((s + 1) // RING + 1), (s + 1) % RING)
                    layer2(g)
                    group_sums(g - 1)
                    layer1(g + 1)
            for g in range((ITERS - 1) * RING + 1, G):
                if g < G - 1:
                    turn_ea(g + 1, ITERS + (1 if g + 1 == G - 1 else 0), (g + 1) % RING)
                layer2(g)
                group_sums(g - 1)
                if g < G - 1:
                    layer1(g + 1)
            group_sums(G - 1)

            def mlp_turn(k, n):
                if k > 1:
                    pe.wait_ge(up.ht, k - 1)
                for j in range(n):
                    last = pe.transpose(pa[:, k % 2, j * P:(j + 1) * P], agg_lin[:, k * RB + j, :], ident[:, :])
                last.then_inc(up.turned, 1)

            def mlp_up(k, n):
                pe.wait_ge(up.ht, k + 1)
                if k > 1:
                    pe.wait_ge(up.out, k - 1)
                pe.matmul(pb[:, k % 2, 0:n * P], wn1_sb[:, :], bt[k % 2][:, 0:n, :].rearrange("p b q -> p (b q)"),
                          start=True, stop=True).then_inc(up.mm, 1)

            def mlp_down(k, n):
                pe.wait_ge(up.out, k + 1)
                if k > 1:
                    pe.wait_ge(down.out, k - 1)
                for j in range(n):
                    last = pe.matmul(mlp_out[k % 2][:, j * F:(j + 1) * F], hid[k % 2][:, j, :], wn2_sb[:, :],
                                     start=True, stop=True)
                last.then_inc(down.mm, 1)

            blocks_of = [RB] * BATCHES + [1]
            pe.reg_add(pairs, pairs, 1)
            pe.wait_ge(lin.added, pairs)
            pe.sem_inc(passed, 1)
            mlp_turn(0, blocks_of[0])
            mlp_turn(1, blocks_of[1])
            mlp_up(0, blocks_of[0])
            for k, n in enumerate(blocks_of):
                if k + 2 <= BATCHES:
                    mlp_turn(k + 2, blocks_of[k + 2])
                if k + 1 <= BATCHES:
                    mlp_up(k + 1, blocks_of[k + 1])
                mlp_down(k, n)


_INS = ['x', 'src', 'dst', 'edge_attr_64', 'L0_gnn_W1', 'L0_gnn_b1', 'L0_gnn_W2', 'L0_gnn_b2', 'L1_gnn_We1', 'L1_gnn_be1',
        'L1_gnn_We2', 'L1_gnn_be2', 'L1_gnn_Wlin', 'L1_gnn_Wn1', 'L1_gnn_bn1', 'L1_gnn_Wn2', 'L1_gnn_bn2']


def kernel(**inputs):
    import numpy as _np
    import concourse.bacc as _bacc
    from concourse import mybir as _mybir
    from concourse.bass_utils import run_bass_kernel_spmd as _run

    nc = _bacc.Bacc("TRN2", target_bir_lowering=False, num_devices=1)
    arrays, args = {}, []
    for name in _INS:
        a = _np.ascontiguousarray(inputs[name])
        arrays[f"in_{name}_dram"] = a
        args.append(nc.dram_tensor(f"in_{name}_dram", a.shape, _mybir.dt.from_np(a.dtype), kind="ExternalInput").ap())
    args.append(nc.dram_tensor("out_dram", (N_NODES, F), _mybir.dt.float32, kind="ExternalOutput").ap())
    gnn_kernel(nc, *args)
    r = _run(nc, [arrays], core_ids=[0])
    return r.results[0]["out_dram"]
```
